# Optimizing a Trainium2 kernel written in Bass

```python
import numpy as np
import jax
import jax.numpy as jnp

def _softmax(x, axis=-1):
    return jax.nn.softmax(x, axis=axis)

def _gelu(x):
    return jax.nn.gelu(x, approximate=True)

def _silu(x):
    return jax.nn.silu(x)

def _sigmoid(x):
    return jax.nn.sigmoid(x)

def _layernorm(x, axis=-1, eps=1e-05):
    m = jnp.mean(x, axis=axis, keepdims=True)
    v = jnp.var(x, axis=axis, keepdims=True)
    return (x - m) / jnp.sqrt(v + eps)

def _scatter_add(tgt, idx, src, axis=0):
    return tgt.at[idx].add(src)

def _segment_sum(src, seg, n):
    return jax.ops.segment_sum(src, seg, n)
kernel_name = 'mk_cond_resid_d2_seqx_r2_ee6db1'

def setup_inputs(seed: int=0):
    np.random.seed(seed)
    _w = jnp.asarray

    def _rec_inputs():
        import jax
        import jax.numpy as jnp
        _rk = jax.random.key(seed)
        x = 7.22e-05 + 1 * jax.random.normal(jax.random.fold_in(_rk, 1), (32, 128, 512), jnp.float32)
        _lenS = 128 - jax.random.randint(jax.random.fold_in(_rk, 7), (32,), 0, max(1, 128 // 4) + 1, jnp.int32)
        _lenS2 = 128 - jax.random.randint(jax.random.fold_in(_rk, 8), (32,), 0, max(1, 128 // 4) + 1, jnp.int32)
        cond_64 = -0.104238 + 1.01173 * jax.random.normal(jax.random.fold_in(_rk, 11), (32, 64), jnp.float32)
        fside_16xSxS_0 = -5.72187e-05 + 0.999849 * jax.random.normal(jax.random.fold_in(_rk, 12), (16, 128, 128), jnp.float32)
        _validS = jnp.arange(128)[None, :] < _lenS[:, None]
        _validS2 = jnp.arange(128)[None, :] < _lenS2[:, None]
        _causal = jnp.tril(jnp.ones((128, 128), dtype=bool))
        mask_BxS_bk0 = jnp.logical_not(jnp.broadcast_to(_validS[:, :], (32, 128)))
        return (x, cond_64, fside_16xSxS_0, mask_BxS_bk0)
    x, cond_64, fside_16xSxS_0, mask_BxS_bk0 = _rec_inputs()

    def _L0_cond_setup():
        import jax, jax.numpy as jnp
        import numpy as np
        B, S, H = (4, 1024, 512)
        E = 8
        M = 256
        K = 2
        N_SHARED = 2
        SM = M * N_SHARED
        G = 64
        GE_TEMP = 1.0
        ALPHA = 0.001
        SEQ_AUX = True
        NORM_TOPK = True
        COS_TEMP = 0.78
        CONS_ALPHA = 0.01
        LEAKY_SLOPE = 0.01
        EPS_COS = 1e-08

        def _leaky(x):
            return jnp.where(x >= 0, x, LEAKY_SLOPE * x)

        def _moe_forward(hidden_states, g, wt, wg, w_gate, w_up, w_down, sw_gate, sw_up, sw_down):
            b, s, h = hidden_states.shape
            x = hidden_states.reshape(-1, h)
            T = x.shape[0]
            logits_h = x @ wt.T
            logits_g = g @ wg.T
            logits_g = jnp.repeat(logits_g, s, axis=0)
            logits = (logits_h + logits_g / GE_TEMP) / (1.0 + 1.0 / GE_TEMP)
            scores = jax.nn.softmax(logits, axis=-1)
            topk_w, topk_idx = jax.lax.top_k(scores, K)
            if K > 1 and NORM_TOPK:
                topk_w = topk_w / (topk_w.sum(-1, keepdims=True) + 1e-20)
            onehot = jax.nn.one_hot(topk_idx.reshape(b, s * K), E, dtype=jnp.float32)
            ce = onehot.sum(1) / (s * K / E)
            aux_loss = (ce * scores.reshape(b, s, E).mean(1)).sum(1).mean() * ALPHA
            gp = _leaky(jnp.einsum('th,ehm->etm', x, w_gate))
            up = jnp.einsum('th,ehm->etm', x, w_up)
            y_all = jnp.einsum('etm,emh->eth', gp * up, w_down)
            y_sel = y_all[topk_idx, jnp.arange(T)[:, None], :]
            y = (y_sel * topk_w[..., None]).sum(1).reshape(b, s, h)
            p = _leaky(hidden_states @ sw_gate) * (hidden_states @ sw_up) @ sw_down
            y = y + p
            num = jnp.sum(y * p, -1)
            den = jnp.maximum(jnp.linalg.norm(y, axis=-1), EPS_COS) * jnp.maximum(jnp.linalg.norm(p, axis=-1), EPS_COS)
            closs = CONS_ALPHA * jnp.mean(num / den / (1.0 + COS_TEMP))
            return (y, aux_loss + closs)
        key = jax.random.key(seed)
        ks = jax.random.split(key, 12)
        sh = 1.0 / np.sqrt(H)
        sm = 1.0 / np.sqrt(M)
        ssm = 1.0 / np.sqrt(SM)
        sg = 1.0 / np.sqrt(G)
        return {'hidden_states': jax.random.normal(ks[0], (B, S, H), jnp.float32), 'g': jax.random.normal(ks[1], (B, G), jnp.float32), 'wt': jax.random.uniform(ks[2], (E, H), jnp.float32, -sh, sh), 'wg': jax.random.uniform(ks[3], (E, G), jnp.float32, -sg, sg), 'w_gate': jax.random.uniform(ks[4], (E, H, M), jnp.float32, -sh, sh), 'w_up': jax.random.uniform(ks[5], (E, H, M), jnp.float32, -sh, sh), 'w_down': jax.random.uniform(ks[6], (E, M, H), jnp.float32, -sm, sm), 'sw_gate': jax.random.uniform(ks[7], (H, SM), jnp.float32, -sh, sh), 'sw_up': jax.random.uniform(ks[8], (H, SM), jnp.float32, -sh, sh), 'sw_down': jax.random.uniform(ks[9], (SM, H), jnp.float32, -ssm, ssm)}
    _L0_cond_all = _L0_cond_setup()
    _L0_cond_in = {k: v for k, v in _L0_cond_all.items() if k in ('wt', 'wg', 'w_gate', 'w_up', 'w_down', 'sw_gate', 'sw_up', 'sw_down')}
    del _L0_cond_all

    def _L1_cond_setup():
        import jax, jax.numpy as jnp
        import numpy as np
        B, N, DIM, H, DH = (2, 1024, 512, 16, 64)
        INNER = H * DH
        EPS = 1e-05

        def layernorm(x, g):
            mean = jnp.mean(x, axis=-1, keepdims=True)
            var = jnp.var(x, axis=-1, keepdims=True)
            return (x - mean) * jax.lax.rsqrt(var + EPS) * g
        key = jax.random.key(seed)
        ks = jax.random.split(key, 10)
        x = jax.random.normal(ks[0], (B, N, DIM), dtype=jnp.float32)
        attn_bias = jax.random.normal(ks[1], (H, N, N), dtype=jnp.float32)
        mask = jax.random.randint(ks[2], (B, N), 0, 2).astype(bool)
        g_in = jnp.ones((DIM,), dtype=jnp.float32)
        null_attn_bias = jax.random.normal(ks[3], (H,), dtype=jnp.float32)
        null_kv = jax.random.normal(ks[4], (2, DH), dtype=jnp.float32)
        Wq = jax.random.normal(ks[5], (DIM, INNER), dtype=jnp.float32) * 0.02
        Wkv = jax.random.normal(ks[6], (DIM, 2 * DH), dtype=jnp.float32) * 0.02
        Wo = jax.random.normal(ks[7], (INNER, DIM), dtype=jnp.float32) * 0.02
        g_out = jnp.ones((DIM,), dtype=jnp.float32)
        return {'x': x, 'attn_bias': attn_bias, 'mask': mask, 'g_in': g_in, 'null_attn_bias': null_attn_bias, 'null_kv': null_kv, 'Wq': Wq, 'Wkv': Wkv, 'Wo': Wo, 'g_out': g_out}
    _L1_cond_all = _L1_cond_setup()
    _L1_cond_in = {k: v for k, v in _L1_cond_all.items() if k in ('g_in', 'null_attn_bias', 'Wq', 'Wkv', 'Wo', 'g_out')}
    del _L1_cond_all
    return {'x': x, 'cond_64': cond_64, 'fside_16xSxS_0': fside_16xSxS_0, 'mask_BxS_bk0': mask_BxS_bk0, 'L0_cond_wt': _L0_cond_in['wt'], 'L0_cond_wg': _L0_cond_in['wg'], 'L0_cond_w_gate': _L0_cond_in['w_gate'], 'L0_cond_w_up': _L0_cond_in['w_up'], 'L0_cond_w_down': _L0_cond_in['w_down'], 'L0_cond_sw_gate': _L0_cond_in['sw_gate'], 'L0_cond_sw_up': _L0_cond_in['sw_up'], 'L0_cond_sw_down': _L0_cond_in['sw_down'], 'L1_cond_g_in': _L1_cond_in['g_in'], 'L1_cond_null_attn_bias': _L1_cond_in['null_attn_bias'], 'L1_cond_Wq': _L1_cond_in['Wq'], 'L1_cond_Wkv': _L1_cond_in['Wkv'], 'L1_cond_Wo': _L1_cond_in['Wo'], 'L1_cond_g_out': _L1_cond_in['g_out']}

def reference(x, cond_64, fside_16xSxS_0, mask_BxS_bk0, L0_cond_wt, L0_cond_wg, L0_cond_w_gate, L0_cond_w_up, L0_cond_w_down, L0_cond_sw_gate, L0_cond_sw_up, L0_cond_sw_down, L1_cond_g_in, L1_cond_null_attn_bias, L1_cond_Wq, L1_cond_Wkv, L1_cond_Wo, L1_cond_g_out):
    import jax
    import jax.numpy as jnp

    def _L0_cond_ref(hidden_states, g, wt, wg, w_gate, w_up, w_down, sw_gate, sw_up, sw_down):
        import jax, jax.numpy as jnp
        import numpy as np
        B, S, H = (4, 1024, 512)
        E = 8
        M = 256
        K = 2
        N_SHARED = 2
        SM = M * N_SHARED
        G = 64
        GE_TEMP = 1.0
        ALPHA = 0.001
        SEQ_AUX = True
        NORM_TOPK = True
        COS_TEMP = 0.78
        CONS_ALPHA = 0.01
        LEAKY_SLOPE = 0.01
        EPS_COS = 1e-08

        def _leaky(x):
            return jnp.where(x >= 0, x, LEAKY_SLOPE * x)

        def _moe_forward(hidden_states, g, wt, wg, w_gate, w_up, w_down, sw_gate, sw_up, sw_down):
            b, s, h = hidden_states.shape
            x = hidden_states.reshape(-1, h)
            T = x.shape[0]
            logits_h = x @ wt.T
            logits_g = g @ wg.T
            logits_g = jnp.repeat(logits_g, s, axis=0)
            logits = (logits_h + logits_g / GE_TEMP) / (1.0 + 1.0 / GE_TEMP)
            scores = jax.nn.softmax(logits, axis=-1)
            topk_w, topk_idx = jax.lax.top_k(scores, K)
            if K > 1 and NORM_TOPK:
                topk_w = topk_w / (topk_w.sum(-1, keepdims=True) + 1e-20)
            onehot = jax.nn.one_hot(topk_idx.reshape(b, s * K), E, dtype=jnp.float32)
            ce = onehot.sum(1) / (s * K / E)
            aux_loss = (ce * scores.reshape(b, s, E).mean(1)).sum(1).mean() * ALPHA
            gp = _leaky(jnp.einsum('th,ehm->etm', x, w_gate))
            up = jnp.einsum('th,ehm->etm', x, w_up)
            y_all = jnp.einsum('etm,emh->eth', gp * up, w_down)
            y_sel = y_all[topk_idx, jnp.arange(T)[:, None], :]
            y = (y_sel * topk_w[..., None]).sum(1).reshape(b, s, h)
            p = _leaky(hidden_states @ sw_gate) * (hidden_states @ sw_up) @ sw_down
            y = y + p
            num = jnp.sum(y * p, -1)
            den = jnp.maximum(jnp.linalg.norm(y, axis=-1), EPS_COS) * jnp.maximum(jnp.linalg.norm(p, axis=-1), EPS_COS)
            closs = CONS_ALPHA * jnp.mean(num / den / (1.0 + COS_TEMP))
            return (y, aux_loss + closs)
        y, _ = _moe_forward(hidden_states, g, wt, wg, w_gate, w_up, w_down, sw_gate, sw_up, sw_down)
        return y

    def _L1_cond_ref(x, attn_bias, mask, g_in, null_attn_bias, null_kv, Wq, Wkv, Wo, g_out):
        import jax, jax.numpy as jnp
        import numpy as np
        B, N, DIM, H, DH = (2, 1024, 512, 16, 64)
        INNER = H * DH
        EPS = 1e-05

        def layernorm(x, g):
            mean = jnp.mean(x, axis=-1, keepdims=True)
            var = jnp.var(x, axis=-1, keepdims=True)
            return (x - mean) * jax.lax.rsqrt(var + EPS) * g
        b, n, _ = x.shape
        scale = DH ** (-0.5)
        xn = layernorm(x, g_in)
        q = (xn @ Wq).reshape(b, n, H, DH).transpose(0, 2, 1, 3) * scale
        kv = xn @ Wkv
        k, v = (kv[..., :DH], kv[..., DH:])
        nk = jnp.broadcast_to(null_kv[0], (b, 1, DH))
        nv = jnp.broadcast_to(null_kv[1], (b, 1, DH))
        k = jnp.concatenate([nk, k], axis=1)
        v = jnp.concatenate([nv, v], axis=1)
        sim = jnp.einsum('bhid,bjd->bhij', q, k)
        null_col = jnp.broadcast_to(null_attn_bias[:, None, None], (H, n, 1))
        bias = jnp.concatenate([null_col, attn_bias], axis=-1)
        sim = sim + bias
        neg = -jnp.finfo(sim.dtype).max
        j = n + 1
        causal_mask = jnp.triu(jnp.ones((n, j), dtype=bool), k=j - n + 1)
        sim = jnp.where(causal_mask, neg, sim)
        mask_p = jnp.pad(mask, ((0, 0), (1, 0)), constant_values=True)
        sim = jnp.where(mask_p[:, None, None, :], sim, neg)
        attn = jax.nn.softmax(sim, axis=-1)
        out = jnp.einsum('bhij,bjd->bhid', attn, v)
        out = out.transpose(0, 2, 1, 3).reshape(b, n, INNER)
        out = out @ Wo
        return layernorm(out, g_out)
    x = x + _L0_cond_ref(x, cond_64, L0_cond_wt, L0_cond_wg, L0_cond_w_gate, L0_cond_w_up, L0_cond_w_down, L0_cond_sw_gate, L0_cond_sw_up, L0_cond_sw_down)
    x = x + _L1_cond_ref(x, fside_16xSxS_0, mask_BxS_bk0, L1_cond_g_in, L1_cond_null_attn_bias, cond_64, L1_cond_Wq, L1_cond_Wkv, L1_cond_Wo, L1_cond_g_out)
    return x

_drawn_inputs = setup_inputs


def setup_inputs(seed=0):
    import zlib

    import numpy as np

    out = dict(_drawn_inputs(seed))
    spreads = {'L1_cond_g_in': (1.0, 0.2), 'L1_cond_g_out': (1.0, 0.2)}
    factors = {}
    for name, (base, spread) in spreads.items():
        noise = np.random.default_rng([zlib.crc32(name.encode()), seed]).standard_normal(out[name].shape)
        drawn = base * np.exp(spread * noise) if base else spread * noise
        out[name] = jnp.asarray(drawn.astype(out[name].dtype))
    for name, factor in factors.items():
        out[name] = (out[name] * factor).astype(out[name].dtype)
    return out
```

```python
from contextlib import ExitStack

import concourse.bass as bass
from concourse import mybir

ALU = mybir.AluOpType
ACT = mybir.ActivationFunctionType
AX = mybir.AxisListType
F32 = mybir.dt.float32
F32R = mybir.dt.float32r
BF16 = mybir.dt.bfloat16
I32 = mybir.dt.int32
U8 = mybir.dt.uint8

P = 128
NEG = -1.0e38
TINY = 1e-20
EPS = 1e-5
LEAK = 0.01


def since(eng, sem, count):
    if isinstance(count, int) and count <= 0:
        return
    eng.wait_ge(sem, count)


def quads(eng, n, body):
    for s in range(4):
        body(0, s)
    with eng.Fori(1, n // 4 - 1) as i:
        for s in range(4):
            body(i, s)
    for s in range(4):
        body(n // 4 - 1, s)


def split3(pe, out, stat, mov, start, stop):
    (sh, sl), (mh, ml) = stat, mov
    pe.matmul(out, sh, mh, start=start, stop=False)
    pe.matmul(out, sh, ml, start=False, stop=False)
    return pe.matmul(out, sl, mh, start=False, stop=stop)


def moe_attention(nc, x, cond, fside, mask, wt, wg, w_gate, w_up, w_down, sw_gate, sw_up, sw_down,
                  g_in, null_bias, wq, wkv, wo, g_out, out):
    NB, S, H = x.shape
    E, _, M = w_gate.shape
    G = cond.shape[1]
    SM = sw_gate.shape[1]
    KC = H // P
    MC = M // P
    NT = NB * S
    NSLOT = 2 * NT // P + E
    NSLOT = (NSLOT + 3) // 4 * 4
    MAXT = NT // P

    x_flat = x.rearrange("b s h -> (b s) h")
    mix_dram = nc.dram_tensor("mix_dram", (NT, H), F32, kind="Internal").ap()
    ids_dram = nc.dram_tensor("ids_dram", (NSLOT * P, 1), F32, kind="Internal").ap()
    ys_dram = nc.dram_tensor("ys_dram", (NSLOT * P, H), F32, kind="Internal").ap()

    base = (nc.sbuf_base + 31) // 32 * 32
    end = nc.sbuf_usable_end
    ctx = ExitStack()
    arena = ctx.enter_context(nc.sbuf_tensor("arena", [P, (end - base) // 32 * 32 - 64], U8))
    cursor = {}

    def region(name, at):
        cursor[name] = [at, at]

    def sb(where, name, shape, dt):
        size = {F32: 4, F32R: 4, I32: 4, BF16: 2, U8: 1}[dt]
        for d in shape[1:]:
            size *= d
        t = nc.alloc_sbuf_tensor_at(name, shape, dt, offset=cursor[where][1])
        cursor[where][1] += (size + 31) // 32 * 32
        assert cursor[where][1] <= end, (name, cursor[where][1] - end)
        return t

    EXPERT_BYTES = E * (KC * 2 * M + MC * H) * 4
    WORK_BYTES, ROUTE_BYTES = 44 * 1024, 14 * 1024 + 512
    SHARED_BYTES = 2 * (KC * 2 * SM + SM // P * H) * 4
    region("experts", base)
    region("stage", base)
    region("shared", base + EXPERT_BYTES)
    region("work", base + EXPERT_BYTES + SHARED_BYTES)
    region("route", base + EXPERT_BYTES + SHARED_BYTES + WORK_BYTES)
    region("tiny", base + EXPERT_BYTES + SHARED_BYTES + WORK_BYTES + ROUTE_BYTES)
    region("attn_a", cursor["experts"][0])
    region("attn_w", cursor["shared"][0])
    region("attn_b", cursor["work"][0])
    region("attn_c", cursor["route"][0])

    wgu = sb("experts", "wgu", [P, E, KC, 2 * M], F32)
    wdn = sb("experts", "wdn", [P, E, MC, H], F32)
    raw = [sb("stage", f"raw{j}", [P, KC, SM], F32) for j in range(3)]
    sh_w = [[sb("shared", f"sw{j}{half}", [P, KC, SM], F32R) for half in "hl"] for j in range(3)]

    xb = sb("work", "xb", [P, 4, H], F32)
    xT0 = sb("work", "xT0", [P, 2, KC, P], F32)
    region("prep", cursor["work"][1])
    xTh = sb("work", "xTh", [P, 2, KC, P], F32R)
    xTl = sb("work", "xTl", [P, 2, KC, P], F32R)
    act_h = sb("work", "act_h", [P, 2, SM], F32)
    hTh = sb("work", "hTh", [P, KC, P], F32R)
    hTl = sb("work", "hTl", [P, KC, P], F32R)
    prep_end = cursor["work"][1]
    mixb = sb("work", "mixb", [P, 2, H], F32)
    eact = sb("work", "eact", [P, 2, M], F32)
    ehT = sb("work", "ehT", [P, 2, MC, P], F32)

    ident = sb("tiny", "ident", [P, P], F32)
    below = sb("route", "below", [P, P], BF16)
    ones_b = sb("route", "ones_b", [P, P], BF16)
    ones_f = sb("route", "ones_f", [NB, P], F32)
    tok = sb("tiny", "tok", [P, NB], F32)
    rank8 = sb("route", "rank8", [P, E], F32)
    steps128 = sb("route", "steps128", [P, MAXT - 1], F32)
    slots = sb("route", "slots", [P, NSLOT], F32)
    zeros = sb("tiny", "zeros", [P, P], F32)
    wt_row = sb("route", "wt_row", [E, H], F32)
    wg_row = sb("route", "wg_row", [E, G], F32)
    cond_row = sb("route", "cond_row", [NB, G], F32)
    wtT = sb("route", "wtT", [P, KC, E], F32)
    wgT = sb("route", "wgT", [G, E], F32)
    condT = sb("route", "condT", [G, NB], F32)
    glog = sb("route", "glog", [NB, E], F32)
    gdiag = sb("route", "gdiag", [NB, NB, E], F32)
    r = {k: sb("route", "r_" + k, [P, NB, E], F32) for k in ("logit", "oh1", "oh2", "a", "b")}
    picks = sb("route", "picks", [P, NB, E], BF16)
    c = {k: sb("tiny", "c_" + k, [P, NB], F32) for k in ("max1", "max2", "t", "sum", "w1", "w2", "p")}
    small = {k: sb("route", "s_" + k, [P, E], F32) for k in ("n", "tiles", "ends", "base", "z")}
    many = sb("route", "many", [P, E, MAXT - 1], F32)
    per_slot = sb("route", "per_slot", [P, NSLOT, E - 1], F32)
    pos = sb("tiny", "pos", [P, NB, 2], I32)
    e_of_slot = sb("tiny", "e_of_slot", [P, 4 + NSLOT], I32)
    cur_pos = sb("tiny", "cur_pos", [P, 4, 2], I32)
    cur_tok = sb("tiny", "cur_tok", [P, 4, 1], F32)
    id_row = sb("tiny", "id_row", [NSLOT, P], F32)
    idx = sb("tiny", "idx", [P, NSLOT], I32)
    cur_idx = sb("tiny", "cur_idx", [P, 4, 1], I32)
    yb = mixb

    NH = null_bias.shape[0]
    D = G
    QC = NH * D // P
    KW = 2 * D + D + NH
    woh, wol = (sb("attn_a", f"wo_{half}", [P, QC, H], F32R) for half in "hl")
    qTh, qTl = (sb("attn_a", f"qT_{half}", [P, 2, QC, 2 * P], F32R) for half in "hl")
    xnh, xnl = (sb("attn_a", f"xnT_{half}", [P, 2, KC, 2 * P], F32R) for half in "hl")
    region("wo_raw", cursor["attn_a"][1])
    wo_raw = sb("wo_raw", "wo_raw", [P, QC, H], F32)
    pTh, pTl = (sb("attn_a", f"pT_{half}", [P, NH, P], F32R) for half in "hl")
    wqh, wql = (sb("attn_w", f"wq_{half}", [P, KC, NH * D], F32R) for half in "hl")
    wkh, wkl = (sb("attn_w", f"wk_{half}", [P, KC, KW], F32R) for half in "hl")
    region("wq_raw", cursor["attn_w"][1])
    wq_raw = sb("wq_raw", "wq_raw", [P, 2, NH * D], F32)
    vzh, vzl = (sb("attn_w", f"vz_{half}", [P, 4, 4, D], F32R) for half in "hl")
    x1 = sb("attn_b", "x1", [P, 2, H], F32)
    y1 = sb("attn_b", "y1", [P, 2, H], F32)
    y2 = sb("attn_b", "y2", [P, 2, H], F32)
    resid = sb("attn_b", "resid", [P, 2, H], F32)
    ob = sb("attn_b", "ob", [P, 2, H], F32)
    kzh, kzl = (sb("attn_b", f"kz_{half}", [P, 2, 2, 2, P], F32R) for half in "hl")
    oTh, oTl = (sb("attn_b", f"oT_{half}", [P, QC, P], F32R) for half in "hl")
    prob = sb("attn_b", "prob", [P, NH, P], F32)
    assert cursor["attn_a"][1] <= cursor["shared"][0] and cursor["attn_w"][1] <= cursor["work"][0]
    assert cursor["attn_b"][1] <= cursor["route"][0] and cursor["work"][1] <= cursor["route"][0]
    assert cursor["route"][1] <= cursor["tiny"][0], cursor
    bias = sb("attn_c", "bias", [P, NH, P], F32)
    null_tmp = sb("prep", "null_tmp", [P, NH * D], F32)
    gout = sb("attn_c", "gout", [P, H], F32)
    woxh, woxl = (sb("attn_c", f"wox_{half}", [P, H], F32R) for half in "hl")
    ident_b = sb("tiny", "ident_b", [P, P], BF16)
    mask_in = sb("prep", "mask_in", [NB, P // 4], I32)
    mneg = sb("tiny", "mneg", [P, P], BF16)
    gin = sb("prep", "gin", [P, KC], F32)
    gin8 = sb("prep", "gin8", [P, KC], F32)
    nkb = sb("prep", "nkb", [P, D], F32)
    nvc = sb("prep", "nvc", [P, 1], F32)
    nbb = sb("tiny", "nbb", [P, NH], F32)
    nvsel = sb("attn_c", "nvsel", [P, QC * NH], F32)
    wnull = sb("prep", "wnull", [P, KC, NH], F32)
    wkv_raw = sb("prep", "wkv_raw", [P, KC, 2 * D], F32)
    nln = sb("tiny", "nln", [P, 4, NH], F32)
    a16 = {k: sb("tiny", "a_" + k, [P, NH], F32) for k in ("max", "negm", "shift", "sum", "p0", "tot", "rs")}
    p0pad = sb("attn_w", "p0pad", [P, P], F32)
    p0Th, p0Tl = (sb("attn_w", f"p0T_{half}", [P, P], F32R) for half in "hl")
    ln = {k: sb("tiny", "ln_" + k, [P, n], F32) for k, n in (("st", 6), ("mv", 2), ("ve", 1), ("rs", 1))}
    fl = {k: sb("tiny", "fl_" + k, [P, n], F32) for k, n in (("st", 6), ("mv", 2), ("ve", 1), ("rs", 1))}
    half_neg = sb("tiny", "half_neg", [P, 1], F32)
    eps = sb("tiny", "eps", [P, 1], F32)
    spare = sb("tiny", "spare", [1, 6], F32)
    cur_y = sb("tiny", "cur_y", [P, 4, 2], I32)
    assert cursor["attn_c"][1] <= cursor["tiny"][0] and cursor["prep"][1] <= prep_end
    x1_dram = nc.dram_tensor("x1_dram", (NT, H), F32, kind="Internal").ap()

    ps = [ctx.enter_context(nc.psum_tensor(f"bank{j}", [P, 512], F32)) for j in range(8)]
    T_, H_, L_, D_ = ps[0], ps[1], ps[2], ps[3]
    GB, UB = ps[4:6], ps[6:8]

    names = {}

    def sem(name):
        names[name] = ctx.enter_context(nc.semaphore(name))
        return names[name]

    consts = sem("consts_written")
    small_in = sem("small_inputs_in")
    raw_in = [sem(f"shared_raw_in{j}") for j in range(3)]
    sh_hi, sh_lo = sem("shared_high_split"), sem("shared_low_split")
    prep_t, prep_c = sem("router_weights_turned"), sem("router_weights_copied")
    experts_in = sem("expert_weights_in")
    x_in = [sem(f"x_tile_in{s}") for s in range(4)]
    t0, c0 = sem("p0_turned"), [sem("p0_copied_even"), sem("p0_copied_odd")]
    lg = sem("p0_logits_done")
    route_v, picks_ok, ranks_ok = sem("route_step"), sem("picks_ready"), sem("ranks_done")
    exp_ok, soft_ok = sem("route_exp_done"), sem("route_shift_ready")
    pos_ok = sem("positions_ready")
    ids_zero, ids_row_in, ids_T, idx_ok = sem("ids_cleared"), sem("ids_row_in"), sem("ids_turned"), sem("idx_ready")
    scat_c = sem("scatter_columns_copied")
    scat = [sem(f"scattered{s}") for s in range(4)]
    xt, xhi, xlo = sem("x_turned"), sem("xT_high"), sem("xT_low")
    gd, ud, dd = sem("gate_done"), sem("up_done"), sem("down_done")
    sg, lk, hd = sem("gate_scaled"), sem("leaky_done"), sem("hidden_done")
    ht, hhi, hlo = sem("h_turned"), sem("hT_high"), sem("hT_low")
    mixed = sem("mix_ready")
    mix_out = [sem(f"mix_stored{s}") for s in range(2)]
    gath_c = sem("gather_column_copied")
    gath = [sem(f"gathered{s}") for s in range(4)]
    ext, exc = sem("e_x_turned"), sem("e_xT_copied")
    egu, esg, elk, ehd = sem("e_gate_up_done"), sem("e_gate_scaled"), sem("e_leaky_done"), sem("e_hidden_done")
    eht, ehc, edn, eyc = sem("e_h_turned"), sem("e_hT_copied"), sem("e_down_done"), sem("e_y_copied")
    ys_out = [sem(f"ys_stored{s}") for s in range(2)]

    N_FILLS, N_CONST = 5, 11
    N_SMALL = 3

    a_small, bias_in, wq_in, wo_in = sem("attn_small_in"), sem("bias_in"), [sem("wq_in0"), sem("wq_in1")], sem("wo_in")
    a_const, g8_ok = sem("attn_consts"), sem("gain_scaled")
    wq_hi, wq_lo = sem("wq_high"), sem("wq_low")
    null_s, wn_ok = sem("null_step"), sem("null_weights_ready")
    wk_hi, wk_lo = sem("wk_high"), sem("wk_low")
    nvs_ok, nvw_done, wox_hi, wox_lo = sem("null_value_select"), sem("null_value_done"), sem("wox_high"), sem("wox_low")
    wo_hi, wo_lo = sem("wo_high"), sem("wo_low")
    z_in, x1_out = [sem(f"mix_in{j}") for j in range(2)], [sem(f"x1_stored{j}") for j in range(2)]
    y_in = [sem(f"y_gathered{j}") for j in range(2)]
    rb_in, o_out = [sem(f"resid_in{j}") for j in range(2)], [sem(f"out_stored{j}") for j in range(2)]
    ln_s, ln_ve, ln_rs, xn_ok = sem("norm_in_step"), sem("norm_in_eps"), sem("norm_in_scale"), sem("xn_ready")
    pj, pj_hi, pj_lo = sem("proj_done"), sem("proj_high"), sem("proj_low")
    sim_d, ttr_d = sem("scores_done"), sem("biased_scores_done")
    neg_ok, shift_ok, exp_d = sem("row_max_ready"), sem("null_shift_ready"), sem("exp_done")
    tot_ok, rs_ok, p0_ok, norm_ok = sem("sum_ready"), sem("sum_inverse_ready"), sem("null_prob_ready"), sem("probs_normal")
    pt_d, pt_hi, pt_lo = sem("probs_turned"), sem("probsT_high"), sem("probsT_low")
    pv_d, pv_hi, pv_lo = sem("pv_done"), sem("pv_high"), sem("pv_low")
    wo_d, f_s, f_ve, f_rs, f_n = sem("out_proj_done"), sem("norm_out_step"), sem("norm_out_eps"), sem("norm_out_scale"), sem("norm_out_done")
    f_g, f_o = sem("out_gained"), sem("out_ready")
    block = ctx.enter_context(nc.Block())

    def at(i, s, d):
        return i + (s + d) // 4, (s + d) % 4

    def exists(i, s):
        return not isinstance(i, int) or 0 <= 4 * i + s < NB

    FIRST = 10
    ORDER = (("x", "v", "k", "q0", "q1", "p0"), ("x", "v", "q2", "q3", "p0"))

    def event(i, s, what):
        if not (isinstance(i, int) and i == NB // 4 - 1):
            return FIRST + 22 * i + 11 * (s // 2) + (6 if s % 2 else 0) + ORDER[s % 2].index(what)
        ahead = {"x": 3, "p0": 0}
        done = [(t, w) for t in range(4) for w in ORDER[t % 2] if 4 * i + t + ahead.get(w, 2) < NB]
        return FIRST + 22 * i + done.index((s, what))

    def bank_of(i, s, what):
        return event(i if isinstance(i, int) else 0, s, what) % 2

    def wait_apart(eng, sem, count, word):
        eng.wait_ge(sem, count)
        eng.memset(spare[:, word:word + 1], 0.0)

    N_ASMALL = 7

    def attention_sync(sp):
        sp.wait_ge(edn, NSLOT)
        sp.dma_start(wo_raw[:], wo.rearrange("(c p) n -> p c n", p=P)).then_inc(wo_in, 16)
        sp.wait_ge(null_s, 2 * KC)
        sp.wait_ge(wk_lo, KC)
        sp.dma_start(gout[:], g_out.rearrange("(a h) -> a h", a=1).to_broadcast([P, H])).then_inc(wo_in, 16)

        def load_mix(i, s):
            b, par = 4 * i + s, s % 2
            if not exists(i, s):
                return
            since(sp, xn_ok, b - 1)
            since(sp, x1_out[par], 16 * (2 * i + s // 2))
            sp.dma_start(x1[:, par, :], mix_dram[bass.ts(b, P), :]).then_inc(z_in[par], 16)

        def store_x1(i, s):
            b, par = 4 * i + s, s % 2
            if not exists(i, s):
                return
            sp.wait_ge(ln_s, 4 * b + 2)
            sp.dma_start(x1_dram[bass.ts(b, P), :], x1[:, par, :]).then_inc(x1_out[par], 16)

        def load_resid(i, s):
            b, par = 4 * i + s, s % 2
            since(sp, f_o, b - 1)
            sp.wait_ge(x1_out[par], 16 * (2 * i + s // 2 + 1))
            sp.dma_start(resid[:, par, :], x1_dram[bass.ts(b, P), :]).then_inc(rb_in[par], 16)

        def store_out(i, s):
            b, par = 4 * i + s, s % 2
            if not exists(i, s):
                return
            sp.wait_ge(f_o, b + 1)
            sp.dma_start(out[bass.ds(b, 1)].rearrange("a s h -> (a s) h"), ob[:, par, :]).then_inc(o_out[par], 16)

        load_mix(0, 0)
        load_mix(0, 1)
        for s in range(2):
            store_x1(0, s)
            load_mix(0, s + 2)
        for s in range(2, 4):
            store_x1(0, s)

        def slot(i, s):
            load_mix(*at(i, s, 4))
            load_resid(i, s)
            store_x1(*at(i, s, 4))
            store_out(*at(i, s, -1))

        quads(sp, NB, slot)
        store_out(NB // 4 - 1, 3)
        for j in range(2):
            sp.wait_ge(o_out[j], 16 * (NB // 2))

    def attention_gpsimd(pl):
        pl.wait_ge(bias_in, 16)
        pl.affine_select(out=bias[:], in_=bias[:], compare_op=ALU.is_ge, fill=NEG, base=0,
                         pattern=[[0, NH], [-1, P]], channel_multiplier=1).then_inc(a_const, 1)
        pl.memset(half_neg[:], -0.5).then_inc(a_const, 1)
        pl.memset(eps[:], EPS).then_inc(a_const, 1)
        pl.tensor_copy(ident_b[:], ident[:]).then_inc(a_const, 1)
        pl.wait_ge(edn, NSLOT)
        pl.wait_ge(eyc, NSLOT)
        pl.wait_ge(wq_lo, KC)
        pl.wait_ge(wk_lo, KC)
        pl.wait_ge(null_s, 2 * KC)
        for z in (kzh, kzl, vzh, vzl, woxh, woxl, p0pad):
            pl.memset(z[:].bitcast(F32), 0.0).then_inc(a_const, 1)
        for j in range(2):
            pl.wait_ge(ys_out[j], 16 * (NSLOT // 2))

        def gather(i, s):
            b, par = 4 * i + s, s % 2
            if not exists(i, s):
                return
            if isinstance(b, int) and b >= 2 or not isinstance(b, int):
                if isinstance(i, int) and i == 0:
                    pl.wait_ge(pj, 1 + (b - 2))
                elif isinstance(i, int) and i == 1 and s == 0:
                    pl.wait_ge(pj, 3)
                else:
                    pl.wait_ge(pj, event(*at(i, s, -5), "x") + 1)
            pl.tensor_copy(cur_y[:, s, :], pos[:, bass.ds(b, 1), :].rearrange("p a b -> p (a b)"))
            pl.drain()
            for k, y in enumerate((y1, y2)):
                pl.indirect_dma_start(y[:, par, :], None, ys_dram,
                                      bass.IndirectOffsetOnAxis(ap=cur_y[:, s, k:k + 1], axis=0)).then_inc(y_in[par], 16)

        def scale_in(i, s):
            b = 4 * i + s
            if not exists(i, s):
                return
            pl.wait_ge(ln_s, 4 * b + 4)
            pl.tensor_tensor(ln["ve"][:], ln["mv"][:, 1:2], eps[:], ALU.add).then_inc(ln_ve, 1)
            pl.wait_ge(ln_ve, b + 1)
            pl.tensor_tensor(ln["rs"][:], ln["ve"][:], half_neg[:], ALU.pow).then_inc(ln_rs, 1)

        def normal(i, s, hf):
            b = 4 * i + s
            pl.wait_ge(rs_ok, 2 * b + hf + 1)
            hs = slice(hf * NH // 2, (hf + 1) * NH // 2)
            pl.tensor_tensor(prob[:, hs, :], prob[:, hs, :],
                             a16["rs"][:, hs].unsqueeze(2).to_broadcast([P, NH // 2, P]), ALU.mult).then_inc(norm_ok, 1)

        def finish(i, s):
            b, par = 4 * i + s, s % 2
            if not exists(i, s):
                return
            pl.wait_ge(f_s, 2 * b + 2)
            pl.tensor_tensor(fl["ve"][:], fl["mv"][:, 1:2], eps[:], ALU.add).then_inc(f_ve, 1)
            pl.wait_ge(f_ve, b + 1)
            pl.tensor_tensor(fl["rs"][:], fl["ve"][:], half_neg[:], ALU.pow).then_inc(f_rs, 1)
            pl.wait_ge(f_n, b + 1)
            pl.tensor_tensor(ob[:, par, :], ob[:, par, :], gout[:], ALU.mult).then_inc(f_g, 1)
            pl.wait_ge(f_g, b + 1)
            pl.wait_ge(rb_in[par], 8 * (b - par) + 16)
            pl.tensor_tensor(ob[:, par, :], ob[:, par, :], resid[:, par, :], ALU.add).then_inc(f_o, 1)

        pl.wait_ge(a_const, 11)
        pl.wait_ge(wo_in, 32)
        for s in range(4):
            gather(0, s) if s < 2 else None
        for s in range(4):
            scale_in(0, s)
            if s < 2:
                gather(0, s + 2)

        def slot(i, s):
            gather(*at(i, s, 4))
            normal(i, s, 0)
            normal(i, s, 1)
            finish(*at(i, s, -1))
            scale_in(*at(i, s, 4))

        quads(pl, NB, slot)
        finish(NB // 4 - 1, 3)

    def wq_high(act, k):
        if k == 0:
            act.wait_ge(dd, NB)
        act.wait_ge(g8_ok, 1)
        act.wait_ge(wq_in[k % 2], 16 * (k // 2 + 1))
        act.activation(wqh[:, k, :], wq_raw[:, k % 2, :], ACT.Copy, scale=gin8[:, k:k + 1]).then_inc(wq_hi, 1)
        act.activation(wkh[:, k, 0:2 * D].rearrange("p (a d) -> p a d", a=2),
                       wkv_raw[:, k, 0:D].unsqueeze(1).to_broadcast([P, 2, D]), ACT.Copy, scale=gin[:, k:k + 1])
        act.activation(wkh[:, k, 2 * D:3 * D], wkv_raw[:, k, D:2 * D], ACT.Copy, scale=gin[:, k:k + 1])
        act.wait_ge(null_s, 2 * k + 2)
        act.activation(wkh[:, k, 3 * D:KW], wnull[:, k, :], ACT.Copy).then_inc(wk_hi, 1)

    def wq_low(dve, k):
        if k == 0:
            dve.wait_ge(a_small, 16 * N_ASMALL)
            dve.wait_ge(dd, NB)
            dve.tensor_scalar(gin8[:], gin[:], float(D) ** -0.5, None, ALU.mult).then_inc(g8_ok, 1)
            dve.memset(mneg[:], 0.0).then_inc(g8_ok, 1)
            dve.memset(nvsel[:], 0.0).then_inc(g8_ok, 1)
            dve.wait_ge(g8_ok, 3)
            dve.tensor_scalar(mneg[0:NB, :], mask_in[:].bitcast(U8), -1.0, -NEG, ALU.add, ALU.mult).then_inc(g8_ok, 1)
            for j in range(2):
                ins = dve.tensor_copy(nvsel[j * D:(j + 1) * D, j::NH + 2],
                                      nvc[j * D:(j + 1) * D, :].to_broadcast([D, QC]))
            ins.then_inc(nvs_ok, 1)
        dve.wait_ge(wq_in[k % 2], 16 * (k // 2 + 1))
        since(dve, null_s, 2 * k)
        dve.scalar_tensor_tensor(null_tmp[:].rearrange("p (h d) -> p h d", d=D),
                                 wq_raw[:, k % 2, :].rearrange("p (h d) -> p h d", d=D), gin8[:, k:k + 1],
                                 nkb[:].unsqueeze(1).to_broadcast([P, NH, D]), ALU.mult, ALU.mult).then_inc(null_s, 1)
        dve.wait_ge(null_s, 2 * k + 1)
        dve.tensor_reduce(wnull[:, k, :], null_tmp[:].rearrange("p (h d) -> p h d", d=D), AX.X, ALU.add).then_inc(null_s, 1)
        dve.wait_ge(wq_hi, k + 1)
        dve.scalar_tensor_tensor(wql[:, k, :], wq_raw[:, k % 2, :], gin8[:, k:k + 1], wqh[:, k, :].bitcast(F32),
                                 ALU.mult, ALU.subtract).then_inc(wq_lo, 1)
        dve.wait_ge(wk_hi, k + 1)
        dve.scalar_tensor_tensor(wkl[:, k, 0:2 * D].rearrange("p (a d) -> p a d", a=2),
                                 wkv_raw[:, k, 0:D].unsqueeze(1).to_broadcast([P, 2, D]), gin[:, k:k + 1],
                                 wkh[:, k, 0:2 * D].bitcast(F32).rearrange("p (a d) -> p a d", a=2),
                                 ALU.mult, ALU.subtract)
        dve.scalar_tensor_tensor(wkl[:, k, 2 * D:3 * D], wkv_raw[:, k, D:2 * D], gin[:, k:k + 1],
                                 wkh[:, k, 2 * D:3 * D].bitcast(F32), ALU.mult, ALU.subtract)
        dve.tensor_tensor(wkl[:, k, 3 * D:KW], wnull[:, k, :], wkh[:, k, 3 * D:KW].bitcast(F32),
                          ALU.subtract).then_inc(wk_lo, 1)

    SB = ps[0:4]
    OB = ps[4:6]
    AB = ps[6:8]

    def halves(engine, kind, dst_h, dst_l, src):
        if kind == "h":
            return engine.activation(dst_h, src, ACT.Copy)
        return engine.tensor_tensor(dst_l, src, dst_h.bitcast(F32), ALU.subtract)

    def evacuate(eng, kind):
        mine, done = (pj_hi, pj) if kind == "h" else (pj_lo, pj_hi)

        def bank(m, par):
            eng.wait_ge(done, m + 1)
            return AB[par]

        def x(i, s, m, par):
            q, j = (s // 2) % 2, s % 2
            src = bank(m, par)[:].rearrange("p (k n) -> p k n", k=KC)
            cols = slice(j * P, (j + 1) * P)
            halves(eng, kind, xnh[:, q, :, cols], xnl[:, q, :, cols], src).then_inc(mine, 1)

        def v(i, s, m, par):
            src = bank(m, par)
            vs = src[:, 0:D].unsqueeze(1).to_broadcast([P, 2, D])
            ins = halves(eng, kind, vzh[:, s, 0:4:3, :], vzl[:, s, 0:4:3, :], vs)
            if kind == "l":
                ins = eng.scalar_tensor_tensor(nln[:, s, :], src[:, D:D + NH], -1.0, nbb[:], ALU.mult, ALU.subtract)
            ins.then_inc(mine, 1)

        def k(i, s, m, par):
            src, q = bank(m, par), (s // 2) % 2
            for j in range(2):
                rows = slice(j * D, (j + 1) * D)
                ins = halves(eng, kind, kzh[rows, q, :, j, :], kzl[rows, q, :, j, :],
                             src[rows, 0:2 * P].rearrange("p (b n) -> p b n", b=2))
            ins.then_inc(mine, 1)

        def q(i, s, m, par, c):
            src, pr = bank(m, par), (s // 2) % 2
            halves(eng, kind, qTh[:, pr, 2 * c:2 * c + 2, :], qTl[:, pr, 2 * c:2 * c + 2, :],
                   src[:].rearrange("p (c n) -> p c n", c=2)).then_inc(mine, 1)

        def p0(i, s, m, par):
            halves(eng, kind, p0Th[:], p0Tl[:], bank(m, par)[:, 0:P]).then_inc(mine, 1)

        return x, v, k, q, p0

    def attention_scalar(act):
        act.wait_ge(edn, NSLOT)
        act.wait_ge(a_const, 11)
        act.wait_ge(wo_in, 32)
        act.wait_ge(nvw_done, 1)
        act.activation(woxh[0:NH, :], SB[0][0:NH, :], ACT.Copy).then_inc(wox_hi, 1)
        act.activation(woh[:], wo_raw[:], ACT.Copy).then_inc(wo_hi, 1)
        x, v, k, q, p0 = evacuate(act, "h")

        def exps(i, s, hf):
            b = 4 * i + s
            act.wait_ge(shift_ok, 2 * b + hf + 1)
            for h in range(hf * NH // 2, (hf + 1) * NH // 2):
                act.activation(prob[:, h, :], prob[:, h, :], ACT.Exp, bias=a16["negm"][:, h:h + 1],
                               accum_out=a16["sum"][:, h:h + 1])
            hs = slice(hf * NH // 2, (hf + 1) * NH // 2)
            act.activation(a16["p0"][:, hs], a16["shift"][:, hs], ACT.Exp).then_inc(exp_d, 1)

        def pv(i, s):
            b = 4 * i + s
            if not exists(i, s):
                return
            for m in range(2):
                act.wait_ge(pv_d, 2 * b + m + 1)
                if m == 0:
                    since(act, wo_d, b)
                cs = slice(m * QC // 2, (m + 1) * QC // 2)
                act.activation(oTh[:, cs, :], OB[m][:].rearrange("p (c n) -> p c n", c=QC // 2), ACT.Copy).then_inc(pv_hi, 1)

        def turned(i, s):
            b = 4 * i + s
            for n in range(4):
                act.wait_ge(pt_d, 4 * b + n + 1)
                since(act, pv_d, 2 * b)
                act.activation(pTh[:, 4 * n:4 * n + 4, :], SB[n][:].rearrange("p (h n) -> p h n", h=4), ACT.Copy).then_inc(pt_hi, 1)

        first(act, x, v, k, q)

        def slot(i, s):
            exps(i, s, 0)
            pv(*at(i, s, -1))
            projections(i, s, x, v, lambda *a: None, lambda *a: None, None, False)
            exps(i, s, 1)
            projections(i, s, None, None, k, q, None, True)
            turned(i, s)
            p0(i, s, event(i, s, "p0"), bank_of(i, s, "p0"))

        quads(act, NB, slot)
        pv(NB // 4 - 1, 3)

    def first(eng, x, v, k, q):
        for b in range(2):
            x(0, b, b, b % 2)
        x(0, 2, 2, 0)
        v(0, 0, 3, 1)
        v(0, 1, 4, 0)
        k(0, 0, 5, 1)
        for c in range(4):
            q(0, 0, 6 + c, c % 2, c)

    def projections(i, s, x, v, k, q, p0, late):
        ex = lambda what: (event(i, s, what), bank_of(i, s, what))
        if not late:
            if exists(*at(i, s, 3)):
                x(*at(i, s, 3), *ex("x"))
            if exists(*at(i, s, 2)):
                v(*at(i, s, 2), *ex("v"))
            return
        if exists(*at(i, s, 2)):
            n = at(i, s, 2)
            if s % 2 == 0:
                k(*n, *ex("k"))
                q(*n, *ex("q0"), 0)
                q(*n, *ex("q1"), 1)
            else:
                q(*n, *ex("q2"), 2)
                q(*n, *ex("q3"), 3)

    def attention_vector(dve):
        dve.wait_ge(edn, NSLOT)
        dve.wait_ge(wox_hi, 1)
        dve.tensor_tensor(woxl[0:NH, :], SB[0][0:NH, :], woxh[0:NH, :].bitcast(F32), ALU.subtract).then_inc(wox_lo, 1)
        x, v, k, q, p0 = evacuate(dve, "l")

        def norm_in(i, s):
            b, par = 4 * i + s, s % 2
            if not exists(i, s):
                return
            dve.wait_ge(z_in[par], 8 * (b - par) + 16)
            dve.wait_ge(y_in[par], 16 * (b - par) + 32)
            dve.scalar_tensor_tensor(x1[:, par, :], y1[:, par, :], c["w1"][:, bass.ds(b, 1)], x1[:, par, :],
                                     ALU.mult, ALU.add).then_inc(ln_s, 1)
            dve.wait_ge(ln_s, 4 * b + 1)
            dve.scalar_tensor_tensor(x1[:, par, :], y2[:, par, :], c["w2"][:, bass.ds(b, 1)], x1[:, par, :],
                                     ALU.mult, ALU.add).then_inc(ln_s, 1)
            dve.wait_ge(ln_s, 4 * b + 2)
            dve.bn_stats(ln["st"][:], x1[:, par, :]).then_inc(ln_s, 1)
            wait_apart(dve, ln_s, 4 * b + 3, 5)
            dve.bn_aggr(ln["mv"][:], ln["st"][:]).then_inc(ln_s, 1)
            dve.wait_ge(ln_rs, b + 1)
            dve.tensor_scalar(y1[:, par, :], x1[:, par, :], ln["mv"][:, 0:1], ln["rs"][:, 0:1],
                              ALU.subtract, ALU.mult).then_inc(xn_ok, 1)

        def scores(i, s, hf):
            b = 4 * i + s
            if hf == 0:
                since(dve, pt_d, 4 * b)
            for h in range(hf * NH // 2, (hf + 1) * NH // 2):
                if h % 4 == 0:
                    wait_apart(dve, sim_d, 4 * b + h // 4 + 1, h // 4)
                ins = dve.tensor_tensor_reduce(prob[:, h, :], SB[h // 4][:, (h % 4) * P:(h % 4 + 1) * P], bias[:, h, :],
                                               1.0, -3.0e38, ALU.add, ALU.max, a16["max"][:, h:h + 1])
            ins.then_inc(ttr_d, 1)
            hs = slice(hf * NH // 2, (hf + 1) * NH // 2)
            dve.wait_ge(ttr_d, 2 * b + hf + 1)
            dve.scalar_tensor_tensor(a16["negm"][:, hs], a16["max"][:, hs], -1.0, nln[:, s, hs],
                                     ALU.mult, ALU.min).then_inc(neg_ok, 1)
            dve.wait_ge(neg_ok, 2 * b + hf + 1)
            dve.tensor_tensor(a16["shift"][:, hs], a16["negm"][:, hs], nln[:, s, hs], ALU.subtract).then_inc(shift_ok, 1)

        def sums(i, s, hf):
            b = 4 * i + s
            hs = slice(hf * NH // 2, (hf + 1) * NH // 2)
            dve.wait_ge(exp_d, 2 * b + hf + 1)
            dve.tensor_tensor(a16["tot"][:, hs], a16["sum"][:, hs], a16["p0"][:, hs], ALU.add).then_inc(tot_ok, 1)
            dve.wait_ge(tot_ok, 2 * b + hf + 1)
            dve.reciprocal(a16["rs"][:, hs], a16["tot"][:, hs]).then_inc(rs_ok, 1)
            dve.wait_ge(rs_ok, 2 * b + hf + 1)
            dve.tensor_tensor(p0pad[:, hs], a16["p0"][:, hs], a16["rs"][:, hs], ALU.mult).then_inc(p0_ok, 1)

        def pv(i, s):
            b = 4 * i + s
            if not exists(i, s):
                return
            for m in range(2):
                dve.wait_ge(pv_hi, 2 * b + m + 1)
                cs = slice(m * QC // 2, (m + 1) * QC // 2)
                halves(dve, "l", oTh[:, cs, :], oTl[:, cs, :],
                       OB[m][:].rearrange("p (c n) -> p c n", c=QC // 2)).then_inc(pv_lo, 1)

        def out_stats(i, s):
            b = 4 * i + s
            if not exists(i, s):
                return
            dve.wait_ge(wo_d, b + 1)
            dve.bn_stats(fl["st"][:], OB[0][:]).then_inc(f_s, 1)
            wait_apart(dve, f_s, 2 * b + 1, 4)
            dve.bn_aggr(fl["mv"][:], fl["st"][:]).then_inc(f_s, 1)

        def out_norm(i, s):
            b, par = 4 * i + s, s % 2
            if not exists(i, s):
                return
            dve.wait_ge(f_rs, b + 1)
            since(dve, o_out[par], 8 * (b - par))
            dve.tensor_scalar(ob[:, par, :], OB[0][:], fl["mv"][:, 0:1], fl["rs"][:, 0:1],
                              ALU.subtract, ALU.mult).then_inc(f_n, 1)

        def turned(i, s, n):
            b = 4 * i + s
            dve.wait_ge(pt_hi, 4 * b + n + 1)
            halves(dve, "l", pTh[:, 4 * n:4 * n + 4, :], pTl[:, 4 * n:4 * n + 4, :],
                   SB[n][:].rearrange("p (h n) -> p h n", h=4)).then_inc(pt_lo, 1)

        dve.wait_ge(a_const, 11)
        for s in range(2):
            norm_in(0, s)
        dve.wait_ge(wo_hi, 1)
        dve.tensor_tensor(wol[:], wo_raw[:], woh[:].bitcast(F32), ALU.subtract).then_inc(wo_lo, 1)
        for b in range(2):
            x(0, b, b, b % 2)
        norm_in(0, 2)
        x(0, 2, 2, 0)
        v(0, 0, 3, 1)
        v(0, 1, 4, 0)
        k(0, 0, 5, 1)
        for c_ in range(4):
            q(0, 0, 6 + c_, c_ % 2, c_)
        norm_in(0, 3)

        def slot(i, s):
            scores(i, s, 0)
            scores(i, s, 1)
            pv(*at(i, s, -1))
            projections(i, s, x, v, None, None, None, False)
            sums(i, s, 0)
            if s % 2 == 0 and exists(*at(i, s, 2)):
                k(*at(i, s, 2), event(i, s, "k"), bank_of(i, s, "k"))
            sums(i, s, 1)
            projections(i, s, None, None, lambda *a: None, q, None, True)
            out_stats(*at(i, s, -1))
            turned(i, s, 0)
            turned(i, s, 1)
            out_norm(*at(i, s, -1))
            turned(i, s, 2)
            turned(i, s, 3)
            p0(i, s, event(i, s, "p0"), bank_of(i, s, "p0"))
            norm_in(*at(i, s, 4))

        quads(dve, NB, slot)
        pv(NB // 4 - 1, 3)
        out_stats(NB // 4 - 1, 3)
        out_norm(NB // 4 - 1, 3)

    def attention_tensor(pe):
        pe.wait_ge(wo_in, 32)
        pe.wait_ge(nvs_ok, 1)
        pe.wait_ge(eyc, NSLOT)
        for cc in range(QC):
            mm = pe.matmul(SB[0][0:NH, :], nvsel[:, cc * NH:(cc + 1) * NH], wo_raw[:, cc, :],
                           start=(cc == 0), stop=(cc == QC - 1))
        mm.then_inc(nvw_done, 1)

        def bank(m, par):
            since(pe, pj_lo, m - 1)
            return AB[par]

        def x(i, s, m, par):
            b, j = 4 * i + s, s % 2
            dst = bank(m, par)
            pe.wait_ge(xn_ok, b + 1)
            for kk in range(KC):
                mm = pe.transpose(dst[:, kk * P:(kk + 1) * P], y1[:, j, kk * P:(kk + 1) * P], ident[:])
            mm.then_inc(pj, 1)

        def v(i, s, m, par):
            q_, cols = (s // 2) % 2, slice((s % 2) * P, (s % 2 + 1) * P)
            dst = bank(m, par)
            pe.wait_ge(pj_lo, m - 2 if isinstance(m, int) and m < FIRST else m)
            for kk in range(KC):
                mm = split3(pe, dst[:, 0:D + NH], (xnh[:, q_, kk, cols], xnl[:, q_, kk, cols]),
                            (wkh[:, kk, 2 * D:KW], wkl[:, kk, 2 * D:KW]), kk == 0, kk == KC - 1)
            mm.then_inc(pj, 1)

        def columns(dst, w, q_):
            for kk in range(KC):
                mm = split3(pe, dst, (w[0][:, kk, :], w[1][:, kk, :]), (xnh[:, q_, kk, :], xnl[:, q_, kk, :]),
                            kk == 0, kk == KC - 1)
            return mm

        def k(i, s, m, par):
            dst = bank(m, par)
            columns(dst[:, 0:2 * P], (wkh[:, :, 0:2 * D], wkl[:, :, 0:2 * D]), (s // 2) % 2).then_inc(pj, 1)

        def q(i, s, m, par, cc):
            dst = bank(m, par)
            for j in range(2):
                cols = slice((2 * cc + j) * P, (2 * cc + j + 1) * P)
                mm = columns(dst[:, j * 2 * P:(j + 1) * 2 * P], (wqh[:, :, cols], wql[:, :, cols]), (s // 2) % 2)
            mm.then_inc(pj, 1)

        def scores(i, s):
            b, q_, j = 4 * i + s, (s // 2) % 2, s % 2
            cols = slice(j * P, (j + 1) * P)
            if s % 2 == 0:
                if isinstance(i, int) and i == 0 and s == 0:
                    pe.wait_ge(pj_lo, FIRST)
                else:
                    pe.wait_ge(pj_lo, event(*at(i, s, -1), "q3") + 1)
            for n in range(4):
                since(pe, pt_lo, 4 * b - 3 + n)
                pe.matmul(SB[n][:], ident_b[:, bass.ds(b, 1)].to_broadcast([P, P]),
                          mneg[:].unsqueeze(1).to_broadcast([P, 4, P]), start=True, stop=False)
                for cc in (2 * n, 2 * n + 1):
                    mm = split3(pe, SB[n][:, (cc % 2) * 2 * P:(cc % 2 + 1) * 2 * P],
                                (qTh[:, q_, cc, cols], qTl[:, q_, cc, cols]),
                                (kzh[:, q_, j].rearrange("p a n -> p (a n)"), kzl[:, q_, j].rearrange("p a n -> p (a n)")),
                                False, cc % 2 == 1)
                mm.then_inc(sim_d, 1)

        def turn_probs(i, s):
            b = 4 * i + s
            for n in range(4):
                if n % 2 == 0:
                    pe.wait_ge(norm_ok, 2 * b + n // 2 + 1)
                for h in range(4 * n, 4 * n + 4):
                    mm = pe.transpose(SB[n][:, (h % 4) * P:(h % 4 + 1) * P], prob[:, h, :], ident[:])
                mm.then_inc(pt_d, 1)
            m, par = event(i, s, "p0"), bank_of(i, s, "p0")
            dst = bank(m, par)
            pe.wait_ge(p0_ok, 2 * b + 2)
            pe.transpose(dst[:, 0:P], p0pad[:], ident[:]).then_inc(pj, 1)

        def pv(i, s):
            b = 4 * i + s
            if not exists(i, s):
                return
            for m in range(2):
                since(pe, pv_lo, 2 * b - 1 + m)
                if m == 0:
                    since(pe, f_n, b)
                pe.wait_ge(pt_lo, 4 * b + 2 * m + 2)
                for j in range(2):
                    hs = slice(8 * m + j, 8 * m + 8, 2)
                    mm = split3(pe, OB[m][:], (vzh[:, s, 2 * j:2 * j + 2, :].rearrange("p a d -> p (a d)"),
                                               vzl[:, s, 2 * j:2 * j + 2, :].rearrange("p a d -> p (a d)")),
                                (pTh[:, hs, :], pTl[:, hs, :]), j == 0, j == 1)
                mm.then_inc(pv_d, 1)

        def out_projection(i, s):
            b = 4 * i + s
            if not exists(i, s):
                return
            pe.wait_ge(pv_lo, 2 * b + 2)
            if isinstance(i, int) and i == 0 and s == 0:
                pe.wait_ge(wo_lo, 1)
                pe.wait_ge(wox_lo, 1)
            pe.wait_ge(pj_lo, event(i, s, "p0") + 1)
            for cc in range(QC):
                split3(pe, OB[0][:], (oTh[:, cc, :], oTl[:, cc, :]), (woh[:, cc, :], wol[:, cc, :]), cc == 0, False)
            split3(pe, OB[0][:], (p0Th[:], p0Tl[:]), (woxh[:], woxl[:]), False, True).then_inc(wo_d, 1)

        pe.wait_ge(wq_lo, KC)
        pe.wait_ge(wk_lo, KC)
        pe.wait_ge(g8_ok, 4)
        first(pe, x, v, k, q)

        def slot(i, s):
            scores(i, s)
            pv(*at(i, s, -1))
            projections(i, s, x, v, None, None, None, False)
            projections(i, s, None, None, k, q, None, True)
            out_projection(*at(i, s, -1))
            turn_probs(i, s)

        quads(pe, NB, slot)
        pv(NB // 4 - 1, 3)
        out_projection(NB // 4 - 1, 3)

    @block.gpsimd
    def _(pl):
        pl.memset(ident[:], 0.0).then_inc(consts, 1)
        pl.memset(below[:], 1.0).then_inc(consts, 1)
        pl.memset(ones_b[:], 1.0).then_inc(consts, 1)
        pl.memset(ones_f[:], 1.0).then_inc(consts, 1)
        pl.memset(zeros[:], 0.0).then_inc(consts, 1)
        pl.wait_ge(consts, N_FILLS)
        pl.affine_select(out=ident[:], in_=ident[:], compare_op=ALU.not_equal, fill=1.0, base=0,
                         pattern=[[-1, P]], channel_multiplier=1).then_inc(consts, 1)
        pl.affine_select(out=below[:], in_=below[:], compare_op=ALU.is_gt, fill=0.0, base=0,
                         pattern=[[1, P]], channel_multiplier=-1).then_inc(consts, 1)
        exact = dict(allow_small_or_imprecise_dtypes=True)
        pl.iota(tok[:], pattern=[[P, NB]], base=0, channel_multiplier=1, **exact).then_inc(consts, 1)
        pl.iota(rank8[:], pattern=[[-1, E]], base=E, channel_multiplier=0, **exact).then_inc(consts, 1)
        pl.iota(steps128[:], pattern=[[P, MAXT - 1]], base=P, channel_multiplier=0, **exact).then_inc(consts, 1)
        pl.iota(slots[:], pattern=[[1, NSLOT]], base=0, channel_multiplier=0, **exact).then_inc(consts, 1)
        pl.wait_ge(pos_ok, 1)
        pl.wait_ge(ids_zero, 16)

        def scatter(i, s):
            t = 4 * i + s
            since(pl, scat[s], 32 * i)
            pl.tensor_copy(cur_pos[:, s, :], pos[:, bass.ds(t, 1), :].rearrange("p a b -> p (a b)"))
            pl.tensor_copy(cur_tok[:, s, :], tok[:, bass.ds(t, 1)]).then_inc(scat_c, 1)
            pl.drain()
            for k in range(2):
                pl.indirect_dma_start(ids_dram, bass.IndirectOffsetOnAxis(ap=cur_pos[:, s, k:k + 1], axis=0),
                                      cur_tok[:, s, :], None).then_inc(scat[s], 16)

        quads(pl, NB, scatter)

        pl.wait_ge(idx_ok, 1)

        def gather(i, s):
            n = 4 * i + s
            since(pl, ext, n - 3)
            if isinstance(i, int) and i == 0:
                pl.wait_ge(mixed, NB)
            pl.tensor_copy(cur_idx[:, s, :], idx[:, bass.ds(n, 1)]).then_inc(gath_c, 1)
            pl.drain()
            pl.indirect_dma_start(xb[:, s, :], None, x_flat,
                                  bass.IndirectOffsetOnAxis(ap=cur_idx[:, s, :], axis=0)).then_inc(gath[s], 16)

        quads(pl, NSLOT, gather)
        attention_gpsimd(pl)

    @block.sync
    def _(sp):
        sp.dma_start(wt_row[:], wt).then_inc(small_in, 16)
        sp.dma_start(wg_row[:], wg).then_inc(small_in, 16)
        sp.dma_start(cond_row[:], cond).then_inc(small_in, 16)

        def load0(i, s):
            since(sp, t0, 4 * i + s - 3)
            sp.dma_start(xb[:, s, :], x[bass.ds(4 * i + s, 1)].rearrange("a s h -> (a s) h")).then_inc(x_in[s], 16)

        quads(sp, NB, load0)
        sp.wait_ge(consts, N_CONST)
        sp.dma_start(ids_dram.rearrange("(a b) o -> a (b o)", b=P), zeros[0:NSLOT, :]).then_inc(ids_zero, 16)
        for s in range(4):
            sp.wait_ge(t0, NB - 3 + s)
            sp.dma_start(xb[:, s, :], x[s]).then_inc(x_in[s], 16)

        def store_mix(i, s):
            t = 4 * i + s
            sp.wait_ge(mixed, t + 1)
            sp.dma_start(mix_dram[bass.ts(t, P), :], mixb[:, s % 2, :]).then_inc(mix_out[s % 2], 16)
            if not (isinstance(i, int) and i == NB // 4 - 1):
                sp.dma_start(xb[:, s, :], x[bass.ds(t + 4, 1)].rearrange("a s h -> (a s) h")).then_inc(x_in[s], 16)
            elif s == 0:
                for q in range(4):
                    sp.wait_ge(scat[q], 2 * 16 * NB // 4)
                sp.dma_start(id_row[:], ids_dram.rearrange("(a b) o -> a (b o)", b=P)).then_inc(ids_row_in, 16)

        quads(sp, NB, store_mix)

        sp.wait_ge(idx_ok, 1)
        sp.wait_ge(dd, NB)
        sp.dma_start(bias[:], fside.rearrange("h i j -> i h j")).then_inc(bias_in, 16)
        with nc.allow_non_contiguous_dma(reason="columns of a few hundred elements"):
            sp.dma_start(gin[:], g_in.rearrange("(k p) -> p k", p=P)).then_inc(a_small, 16)
            for j in range(2):
                sp.dma_start(nvc[j * D:(j + 1) * D, :], cond[1:2, :].rearrange("a d -> d a")).then_inc(a_small, 16)
        sp.dma_start(nkb[:], cond[0:1, :].to_broadcast([P, D])).then_inc(a_small, 16)
        sp.dma_start(nbb[:], null_bias.rearrange("(a h) -> a h", a=1).to_broadcast([P, NH])).then_inc(a_small, 16)
        sp.dma_start(mask_in[:], mask).then_inc(a_small, 16)
        sp.dma_start(wkv_raw[:], wkv.rearrange("(k p) n -> p k n", p=P)).then_inc(a_small, 16)
        for k in range(2):
            sp.dma_start(wq_raw[:, k, :], wq[k * P:(k + 1) * P, :]).then_inc(wq_in[k], 16)

        def store_y(i, s):
            n = 4 * i + s
            sp.wait_ge(eyc, n + 1)
            sp.dma_start(ys_dram[bass.ts(n, P), :], yb[:, s % 2, :]).then_inc(ys_out[s % 2], 16)

        for s in range(4):
            store_y(0, s)
        for k in range(KC):
            with sp.Fori(1 + 4 * k, 5 + 4 * k) as i:
                for s in range(4):
                    store_y(i, s)
            if k < 2:
                sp.wait_ge(wq_hi, k + 1)
                sp.wait_ge(null_s, 2 * (k + 1))
                sp.dma_start(wq_raw[:, k, :], wq[(k + 2) * P:(k + 3) * P, :]).then_inc(wq_in[k], 16)
        for s in range(4):
            store_y(NSLOT // 4 - 1, s)
        for s in range(2):
            sp.wait_ge(mix_out[s], 16 * (NB // 2))
            sp.wait_ge(ys_out[s], 16 * (NSLOT // 2))
        attention_sync(sp)

    @block.scalar
    def _(act):
        for j, w in enumerate((sw_gate, sw_up, sw_down)):
            act.dma_start(raw[j][:], w.rearrange("(k p) n -> p k n", p=P)).then_inc(raw_in[j], 16)

        def copy0(i, s):
            if s % 2:
                return
            t = 4 * i + s
            since(act, t0, t + 1)
            since(act, lg, t - 1)
            act.activation(xT0[:, 0], ps[s % 2][:].rearrange("p (k n) -> p k n", k=KC), ACT.Copy).then_inc(c0[0], 1)

        quads(act, NB, copy0)
        for j in range(3):
            act.wait_ge(raw_in[j], 16)
            act.activation(sh_w[j][0][:], raw[j][:], ACT.Copy).then_inc(sh_hi, 1)
        act.wait_ge(sh_lo, 3)
        for e in range(E):
            for j, w in enumerate((w_gate, w_up)):
                act.dma_start(wgu[:, e, :, j * M:(j + 1) * M], w[e].rearrange("(k p) m -> p k m", p=P)).then_inc(experts_in, 16)
            act.dma_start(wdn[:, e], w_down[e].rearrange("(k p) n -> p k n", p=P)).then_inc(experts_in, 16)

        def xhigh(n, par):
            since(act, xt, n + 1)
            since(act, ud, n - 1)
            act.activation(xTh[:, par], T_[:].rearrange("p (k n) -> p k n", k=KC), ACT.Copy).then_inc(xhi, 1)

        def step1(i, s):
            n, par = 4 * i + s, s % 2
            last = isinstance(i, int) and n == NB - 1
            if not last:
                xhigh(n + 1, 1 - par)
            since(act, gd, n + 1)
            since(act, ht, n - 1)
            act.activation(act_h[:, par, :], GB[par][:], ACT.Copy, scale=LEAK).then_inc(sg, 1)
            hhigh(n - 1)

        def hhigh(n):
            if isinstance(n, int) and n < 0:
                return
            since(act, ht, n + 1)
            since(act, dd, n)
            act.activation(hTh[:], H_[:].rearrange("p (k n) -> p k n", k=KC), ACT.Copy).then_inc(hhi, 1)

        act.wait_ge(soft_ok, 1)
        act.activation(r["a"][:], r["b"][:], ACT.Exp).then_inc(exp_ok, 1)
        act.activation(c["t"][:], c["p"][:], ACT.Exp).then_inc(exp_ok, 1)
        xhigh(0, 0)
        quads(act, NB, step1)
        hhigh(NB - 1)

        def excopy(n, par):
            since(act, ext, n + 1)
            since(act, egu, n - 1)
            act.activation(xT0[:, par], T_[:].rearrange("p (k n) -> p k n", k=KC), ACT.Copy).then_inc(exc, 1)

        def step2(i, s):
            n, par = 4 * i + s, s % 2
            if not (isinstance(i, int) and n == NSLOT - 1):
                excopy(n + 1, 1 - par)
            since(act, egu, n + 1)
            since(act, eht, n - 1)
            act.activation(eact[:, par, :], GB[par][:, 0:M], ACT.Copy, scale=LEAK).then_inc(esg, 1)
            ycopy(n - 1, 1 - par)

        def ycopy(n, par):
            if isinstance(n, int) and n < 0:
                return
            since(act, edn, n + 1)
            if isinstance(n, int) and n < 2:
                act.wait_ge(mix_out[par], 16 * (NB // 2))
            else:
                act.wait_ge(ys_out[par], 8 * (n - par))
            act.activation(yb[:, par, :], UB[par][:], ACT.Copy).then_inc(eyc, 1)

        excopy(0, 0)
        for s in range(4):
            step2(0, s)
        for k in range(KC):
            with act.Fori(1 + 4 * k, 5 + 4 * k) as i:
                for s in range(4):
                    step2(i, s)
            wq_high(act, k)
        for s in range(4):
            step2(NSLOT // 4 - 1, s)
        ycopy(NSLOT - 1, (NSLOT - 1) % 2)
        attention_scalar(act)

    @block.vector
    def _(dve):
        dve.wait_ge(prep_t, 1)
        dve.tensor_copy(wtT[:], ps[0][:, 0:KC * E].rearrange("p (k e) -> p k e", k=KC)).then_inc(prep_c, 1)
        dve.tensor_copy(wgT[:], ps[1][0:G, 0:E]).then_inc(prep_c, 1)
        dve.tensor_copy(condT[:], ps[1][0:G, E:E + NB]).then_inc(prep_c, 1)

        def copy0(i, s):
            if s % 2 == 0:
                return
            t = 4 * i + s
            since(dve, t0, t + 1)
            since(dve, lg, t - 1)
            dve.tensor_copy(xT0[:, 1], ps[s % 2][:].rearrange("p (k n) -> p k n", k=KC)).then_inc(c0[1], 1)

        quads(dve, NB, copy0)
        for j in range(3):
            dve.wait_ge(sh_hi, j + 1)
            dve.tensor_tensor(sh_w[j][1][:], raw[j][:], sh_w[j][0][:].bitcast(F32), ALU.subtract).then_inc(sh_lo, 1)

        count = [0]

        def link(ins):
            ins.then_inc(route_v, 1)
            count[0] += 1
            dve.wait_ge(route_v, count[0])

        def over_e(v):
            return v.unsqueeze(2).to_broadcast([P, NB, E])

        def over_t(v):
            return v.unsqueeze(1).to_broadcast([P, NB, E])

        logit, oh1, oh2, ta, tb = (r[k][:] for k in ("logit", "oh1", "oh2", "a", "b"))
        dve.wait_ge(consts, N_CONST)
        dve.wait_ge(prep_t, 2)
        link(dve.tensor_copy(glog[:], ps[1][0:NB, 0:E]))
        dve.tensor_tensor(gdiag[:], ident[0:NB, 0:NB].unsqueeze(2).to_broadcast([NB, NB, E]),
                          glog[:].unsqueeze(1).to_broadcast([NB, NB, E]), ALU.mult).then_inc(prep_c, 1)
        dve.wait_ge(prep_t, 3)
        link(dve.tensor_copy(ta, ps[1][:, 0:NB * E].rearrange("p (t e) -> p t e", e=E)))
        link(dve.tensor_tensor(tb, L_[:, 0:NB * E].rearrange("p (t e) -> p t e", e=E), ta, ALU.add))
        link(dve.tensor_scalar(logit, tb, 0.5, None, ALU.mult))

        def first_of(onehot, values, top):
            link(dve.tensor_reduce(top, values, AX.X, ALU.max))
            link(dve.tensor_tensor(ta, values, over_e(top), ALU.is_equal))
            link(dve.tensor_tensor(ta, ta, over_t(rank8[:]), ALU.mult))
            link(dve.tensor_reduce(c["t"][:], ta, AX.X, ALU.max))
            link(dve.tensor_tensor(onehot, ta, over_e(c["t"][:]), ALU.is_equal))

        first_of(oh1, logit, c["max1"][:])
        link(dve.scalar_tensor_tensor(tb, oh1, -3.0e38, logit, ALU.mult, ALU.add))
        first_of(oh2, tb, c["max2"][:])
        dve.tensor_tensor(picks[:], oh1, oh2, ALU.add).then_inc(picks_ok, 1)
        link(dve.tensor_tensor(tb, logit, over_e(c["max1"][:]), ALU.subtract))
        dve.tensor_tensor(c["p"][:], c["max2"][:], c["max1"][:], ALU.subtract).then_inc(soft_ok, 1)

        def xlow(n, par):
            since(dve, xhi, n + 1)
            since(dve, ud, n - 1)
            dve.tensor_tensor(xTl[:, par], T_[:].rearrange("p (k n) -> p k n", k=KC), xTh[:, par].bitcast(F32),
                              ALU.subtract).then_inc(xlo, 1)

        def hlow(n):
            if isinstance(n, int) and n < 0:
                return
            since(dve, hhi, n + 1)
            dve.tensor_tensor(hTl[:], H_[:].rearrange("p (k n) -> p k n", k=KC), hTh[:].bitcast(F32),
                              ALU.subtract).then_inc(hlo, 1)

        def leaky(n, par):
            since(dve, sg, n + 1)
            dve.tensor_tensor(act_h[:, par, :], act_h[:, par, :], GB[par][:], ALU.max).then_inc(lk, 1)

        def hidden(n, par):
            since(dve, ud, n + 1)
            since(dve, lk, n + 1)
            dve.tensor_tensor(act_h[:, par, :], act_h[:, par, :], UB[par][:], ALU.mult).then_inc(hd, 1)

        def mix(n, par, slot):
            if isinstance(n, int) and n < 0:
                return
            since(dve, dd, n + 1)
            if not (isinstance(n, int) and n < 2):
                dve.wait_ge(mix_out[par], 8 * (n - par))
            dve.tensor_tensor(mixb[:, par, :], xb[:, slot, :], D_[:], ALU.add).then_inc(mixed, 1)

        def step1(i, s):
            n, par = 4 * i + s, s % 2
            if not (isinstance(i, int) and n == NB - 1):
                xlow(n + 1, 1 - par)
            leaky(n, par)
            hlow(n - 1)
            hidden(n, par)
            mix(n - 1, 1 - par, (s + 3) % 4)

        def slots_of_tokens():
            dve.wait_ge(exp_ok, 2)
            link(dve.tensor_reduce(c["sum"][:], ta, AX.X, ALU.add))
            link(dve.reciprocal(c["sum"][:], c["sum"][:]))
            link(dve.tensor_tensor(c["w2"][:], c["t"][:], c["sum"][:], ALU.mult))
            link(dve.scalar_tensor_tensor(c["p"][:], c["sum"][:], TINY, c["w2"][:], ALU.add, ALU.add))
            link(dve.reciprocal(c["p"][:], c["p"][:]))
            link(dve.tensor_tensor(c["w1"][:], c["sum"][:], c["p"][:], ALU.mult))
            link(dve.tensor_tensor(c["w2"][:], c["w2"][:], c["p"][:], ALU.mult))
            dve.wait_ge(ranks_ok, 1)
            link(dve.tensor_copy(ta, L_[:, NB * E:2 * NB * E].rearrange("p (t e) -> p t e", e=E)))
            link(dve.memset(small["z"][:], 0.0))
            zero_col = small["z"][:, 0:1].to_broadcast([P, NB])
            for e in range(E):
                step = dve.tensor_tensor_scan(tb[:, :, e], ta[:, :, e], zero_col, 0.0, ALU.add, ALU.add)
            link(step)
            link(dve.tensor_copy(small["n"][:], tb[:, NB - 1, :]))
            link(dve.tensor_tensor(many[:], small["n"][:].unsqueeze(2).to_broadcast([P, E, MAXT - 1]),
                                   steps128[:].unsqueeze(1).to_broadcast([P, E, MAXT - 1]), ALU.is_gt))
            link(dve.tensor_reduce(small["tiles"][:], many[:], AX.X, ALU.add))
            link(dve.tensor_scalar(small["tiles"][:], small["tiles"][:], 1.0, None, ALU.add))
            link(dve.tensor_tensor_scan(small["ends"][:], small["tiles"][:], small["z"][:], 0.0, ALU.add, ALU.add))
            link(dve.tensor_tensor(small["base"][:], small["ends"][:], small["tiles"][:], ALU.subtract))
            link(dve.tensor_scalar(small["base"][:], small["base"][:], float(P), None, ALU.mult))
            link(dve.tensor_tensor(tb, tb, ta, ALU.subtract))
            link(dve.tensor_tensor(ta, tb, over_t(small["base"][:]), ALU.add))
            link(dve.tensor_tensor(tb, ta, L_[:, 0:NB * E].rearrange("p (t e) -> p t e", e=E), ALU.add))
            for k, oh in enumerate((oh1, oh2)):
                link(dve.tensor_tensor(ta, tb, oh, ALU.mult))
                link(dve.tensor_reduce(c["t"][:], ta, AX.X, ALU.add))
                step = dve.tensor_copy(pos[:, :, k], c["t"][:])
                if k:
                    step.then_inc(pos_ok, 1)
                else:
                    link(step)
            link(dve.tensor_tensor(per_slot[:], slots[:].unsqueeze(2).to_broadcast([P, NSLOT, E - 1]),
                                   small["ends"][:, 0:E - 1].unsqueeze(1).to_broadcast([P, NSLOT, E - 1]), ALU.is_ge))
            link(dve.tensor_reduce(many_flat, per_slot[:], AX.X, ALU.add))
            dve.tensor_copy(e_of_slot[:, 4:], many_flat).then_inc(route_v, 1)
            count[0] += 1

        many_flat = many[:].rearrange("p a b -> p (a b)")[:, 0:NSLOT]
        xlow(0, 0)
        for s in range(2):
            step1(0, s)
        slots_of_tokens()
        for s in range(2, 4):
            step1(0, s)
        with dve.Fori(1, NB // 4 - 1) as i:
            for s in range(4):
                step1(i, s)
        for s in range(4):
            step1(NB // 4 - 1, s)
            if s == 2:
                dve.wait_ge(ids_T, 1)
                dve.tensor_copy(idx[:], L_[:, 0:NSLOT]).then_inc(idx_ok, 1)
        hlow(NB - 1)
        mix(NB - 1, (NB - 1) % 2, 3)
        names["route_total"] = count[0]

        def ehcopy(n, par):
            if isinstance(n, int) and n < 0:
                return
            since(dve, eht, n + 1)
            since(dve, edn, n - 1)
            dve.tensor_copy(ehT[:, par], H_[:, 0:M].rearrange("p (k n) -> p k n", k=MC)).then_inc(ehc, 1)

        def step2(i, s):
            n, par = 4 * i + s, s % 2
            ehcopy(n - 1, 1 - par)
            since(dve, esg, n + 1)
            dve.tensor_tensor(eact[:, par, :], eact[:, par, :], GB[par][:, 0:M], ALU.max).then_inc(elk, 1)
            since(dve, elk, n + 1)
            dve.tensor_tensor(eact[:, par, :], eact[:, par, :], GB[par][:, M:2 * M], ALU.mult).then_inc(ehd, 1)

        for s in range(4):
            step2(0, s)
        for k in range(KC):
            with dve.Fori(1 + 4 * k, 5 + 4 * k) as i:
                for s in range(4):
                    step2(i, s)
            wq_low(dve, k)
        for s in range(4):
            step2(NSLOT // 4 - 1, s)
        ehcopy(NSLOT - 1, (NSLOT - 1) % 2)
        attention_vector(dve)

    @block.tensor
    def _(pe):
        pe.wait_ge(consts, N_CONST)
        pe.wait_ge(small_in, 16 * N_SMALL)
        for k in range(KC):
            pe.transpose(ps[0][:, k * E:(k + 1) * E], wt_row[:, k * P:(k + 1) * P], ident[0:E, 0:E])
        pe.transpose(ps[1][0:G, 0:E], wg_row[:], ident[0:E, 0:E])
        pe.transpose(ps[1][0:G, E:E + NB], cond_row[:], ident[0:NB, 0:NB]).then_inc(prep_t, 1)
        pe.wait_ge(prep_c, 3)

        def turn0(i, s):
            t = 4 * i + s
            pe.wait_ge(x_in[s], 16 * (i + 1))
            since(pe, c0[s % 2], 2 * i + s // 2)
            for k in range(KC):
                mm = pe.transpose(ps[s % 2][:, k * P:(k + 1) * P], xb[:, s, k * P:(k + 1) * P], ident[:])
            mm.then_inc(t0, 1)

        def logits0(i, s):
            if isinstance(i, int) and i < 0:
                return
            t = 4 * i + s
            pe.wait_ge(c0[s % 2], 2 * i + s // 2 + 1)
            o = L_[:, bass.ds(t * E, E)]
            for k in range(KC):
                mm = pe.matmul(o, xT0[:, s % 2, k, :], wtT[:, k, :], start=(k == 0), stop=(k == KC - 1))
            mm.then_inc(lg, 1)

        def step0(i, s):
            turn0(i, s)
            if s:
                logits0(i, s - 1)
            else:
                logits0(i - 1, 3)

        quads(pe, NB, step0)
        logits0(NB // 4 - 1, 3)
        pe.wait_ge(c0[1], NB // 2)
        pe.matmul(ps[1][0:NB, 0:E], condT[:], wgT[:], start=True, stop=True).then_inc(prep_t, 1)
        pe.wait_ge(prep_c, 4)
        pe.matmul(ps[1][:, 0:NB * E], ones_f[:], gdiag[:].rearrange("p t e -> p (t e)"),
                  start=True, stop=True).then_inc(prep_t, 1)
        pe.wait_ge(route_v, 2)

        def turn(i, s):
            n = 4 * i + s
            pe.wait_ge(x_in[s], 16 * (NB // 4 + i + 1))
            since(pe, xlo, n)
            if isinstance(n, int) and n == 0:
                pe.wait_ge(c0[0], NB // 2)
            for k in range(KC):
                mm = pe.transpose(T_[:, k * P:(k + 1) * P], xb[:, s, k * P:(k + 1) * P], ident[:])
            mm.then_inc(xt, 1)

        def turn_h(n, par):
            if isinstance(n, int) and n < 0:
                return
            since(pe, hd, n + 1)
            since(pe, hlo, n)
            for k in range(KC):
                mm = pe.transpose(H_[:, k * P:(k + 1) * P], act_h[:, par, k * P:(k + 1) * P], ident[:])
            mm.then_inc(ht, 1)

        def project(bank, par, w):
            for k in range(KC):
                mm = split3(pe, bank[:], (xTh[:, par, k], xTl[:, par, k]), (w[0][:, k], w[1][:, k]),
                            k == 0, k == KC - 1)
            return mm

        def down(n):
            if isinstance(n, int) and n < 0:
                return
            since(pe, hlo, n + 1)
            since(pe, mixed, n)
            for k in range(KC):
                mm = split3(pe, D_[:], (hTh[:, k], hTl[:, k]), (sh_w[2][0][:, k], sh_w[2][1][:, k]),
                            k == 0, k == KC - 1)
            mm.then_inc(dd, 1)

        def step1(i, s):
            n, par = 4 * i + s, s % 2
            if not (isinstance(i, int) and n == NB - 1):
                turn(i + (s == 3), (s + 1) % 4)
            since(pe, xlo, n + 1)
            since(pe, lk, n - 1)
            project(GB[par], par, sh_w[0]).then_inc(gd, 1)
            turn_h(n - 1, 1 - par)
            since(pe, hd, n - 1)
            project(UB[par], par, sh_w[1]).then_inc(ud, 1)
            down(n - 1)

        pe.wait_ge(sh_lo, 3)
        turn(0, 0)
        for s in range(4):
            step1(0, s)
            if s == 0:
                pe.wait_ge(picks_ok, 1)
                pe.matmul(L_[:, 0:NB * E], below[:], picks[:].rearrange("p t e -> p (t e)"), start=True, stop=True)
                pe.matmul(L_[:, NB * E:2 * NB * E], ones_b[:], picks[:].rearrange("p t e -> p (t e)"),
                          start=True, stop=True).then_inc(ranks_ok, 1)
        with pe.Fori(1, NB // 4 - 1) as i:
            for s in range(4):
                step1(i, s)
        for s in range(4):
            step1(NB // 4 - 1, s)
            if s == 1:
                pe.wait_ge(ids_row_in, 16)
                pe.transpose(L_[:, 0:NSLOT], id_row[:], ident[0:NSLOT, 0:NSLOT]).then_inc(ids_T, 1)
        turn_h(NB - 1, (NB - 1) % 2)
        down(NB - 1)

        def eturn(i, s):
            n = 4 * i + s
            pe.wait_ge(gath[s], 16 * (i + 1))
            since(pe, exc, n)
            for k in range(KC):
                mm = pe.transpose(T_[:, k * P:(k + 1) * P], xb[:, s, k * P:(k + 1) * P], ident[:])
            mm.then_inc(ext, 1)

        def eturn_h(n, par):
            if isinstance(n, int) and n < 0:
                return
            since(pe, ehd, n + 1)
            since(pe, ehc, n)
            for k in range(MC):
                mm = pe.transpose(H_[:, k * P:(k + 1) * P], eact[:, par, k * P:(k + 1) * P], ident[:])
            mm.then_inc(eht, 1)

        def edown(n, par, e):
            if isinstance(n, int) and n < 0:
                return
            since(pe, ehc, n + 1)
            since(pe, eyc, n - 1)
            for k in range(MC):
                mm = pe.matmul(UB[par][:], ehT[:, par, k], wdn[:, bass.ds(e, 1), k, :].rearrange("p a n -> p (a n)"),
                               start=(k == 0), stop=(k == MC - 1))
            mm.then_inc(edn, 1)

        def expert(n):
            return pe.value_load(e_of_slot[0:1, bass.ds(4 + n, 1)], min_val=0, max_val=E - 1)

        def step2(i, s, e_prev):
            n, par = 4 * i + s, s % 2
            if not (isinstance(i, int) and n == NSLOT - 1):
                eturn(i + (s == 3), (s + 1) % 4)
            e = expert(n)
            if s == 0 and not (isinstance(i, int) and i == 0):
                e_prev = expert(n - 1)
            since(pe, exc, n + 1)
            since(pe, ehd, n - 1)
            for k in range(KC):
                if k == KC // 2:
                    eturn_h(n - 1, 1 - par)
                mm = pe.matmul(GB[par][:], xT0[:, par, k], wgu[:, bass.ds(e, 1), k, :].rearrange("p a n -> p (a n)"),
                               start=(k == 0), stop=(k == KC - 1))
            mm.then_inc(egu, 1)
            edown(n - 1, 1 - par, e_prev)
            return e

        pe.wait_ge(experts_in, 16 * 3 * E)
        pe.wait_ge(route_v, names["route_total"])
        since(pe, xlo, NB)
        pe.wait_ge(hlo, NB)
        pe.wait_ge(hd, NB)
        eturn(0, 0)
        held = [None]

        def body(i, s):
            held[0] = step2(i, s, held[0])

        quads(pe, NSLOT, body)
        edown_h = (NSLOT - 1) % 2
        eturn_h(NSLOT - 1, edown_h)
        edown(NSLOT - 1, edown_h, held[0])
        attention_tensor(pe)
    ctx.close()


def kernel(x, cond_64, fside_16xSxS_0, mask_BxS_bk0, L0_cond_wt, L0_cond_wg, L0_cond_w_gate, L0_cond_w_up,
           L0_cond_w_down, L0_cond_sw_gate, L0_cond_sw_up, L0_cond_sw_down, L1_cond_g_in,
           L1_cond_null_attn_bias, L1_cond_Wq, L1_cond_Wkv, L1_cond_Wo, L1_cond_g_out):
    import numpy as np

    import concourse.bacc as bacc
    from concourse.bass_utils import run_bass_kernel_spmd

    arrays = {"x": x, "cond": cond_64, "attn_bias": fside_16xSxS_0, "mask": np.ascontiguousarray(mask_BxS_bk0).view(np.int32),
              "wt": L0_cond_wt, "wg": L0_cond_wg, "w_gate": L0_cond_w_gate, "w_up": L0_cond_w_up,
              "w_down": L0_cond_w_down, "sw_gate": L0_cond_sw_gate, "sw_up": L0_cond_sw_up,
              "sw_down": L0_cond_sw_down, "g_in": L1_cond_g_in, "null_attn_bias": L1_cond_null_attn_bias,
              "wq": L1_cond_Wq, "wkv": L1_cond_Wkv, "wo": L1_cond_Wo, "g_out": L1_cond_g_out}
    arrays = {name: np.asarray(a) for name, a in arrays.items()}
    nc = bacc.Bacc("TRN2", target_bir_lowering=False, num_devices=1)
    ins = [nc.dram_tensor(f"in_{name}_dram", a.shape, mybir.dt.from_np(a.dtype), kind="ExternalInput").ap()
           for name, a in arrays.items()]
    out = nc.dram_tensor("out_dram", arrays["x"].shape, F32, kind="ExternalOutput").ap()
    moe_attention(nc, *ins, out)
    nc.compile()
    res = run_bass_kernel_spmd(nc, [{f"in_{name}_dram": a for name, a in arrays.items()}], core_ids=[0])
    return res.results[0]["out_dram"]
```

```python
from contextlib import ExitStack

import concourse.bass as bass
from concourse import mybir

ALU = mybir.AluOpType
ACT = mybir.ActivationFunctionType
AX = mybir.AxisListType
F32 = mybir.dt.float32
F32R = mybir.dt.float32r
BF16 = mybir.dt.bfloat16
I32 = mybir.dt.int32
U8 = mybir.dt.uint8

P = 128
NEG = -1.0e38
TINY = 1e-20
EPS = 1e-5
LEAK = 0.01


def since(eng, sem, count):
    if isinstance(count, int) and count <= 0:
        return
    eng.wait_ge(sem, count)


def quads(eng, n, body):
    for s in range(4):
        body(0, s)
    with eng.Fori(1, n // 4 - 1) as i:
        for s in range(4):
            body(i, s)
    for s in range(4):
        body(n // 4 - 1, s)


def split3(pe, out, stat, mov, start, stop):
    (sh, sl), (mh, ml) = stat, mov
    pe.matmul(out, sh, mh, start=start, stop=False)
    pe.matmul(out, sh, ml, start=False, stop=False)
    return pe.matmul(out, sl, mh, start=False, stop=stop)


def moe_attention(nc, x, cond, fside, mask, wt, wg, w_gate, w_up, w_down, sw_gate, sw_up, sw_down,
                  g_in, null_bias, wq, wkv, wo, g_out, out):
    NB, S, H = x.shape
    E, _, M = w_gate.shape
    G = cond.shape[1]
    SM = sw_gate.shape[1]
    KC = H // P
    MC = M // P
    NT = NB * S
    NSLOT = 2 * NT // P + E
    NSLOT = (NSLOT + 3) // 4 * 4
    MAXT = NT // P
    EARLY = 12
    AHEAD = NB - 2 * EARLY

    x_flat = x.rearrange("b s h -> (b s) h")
    mix_dram = nc.dram_tensor("mix_dram", (NT, H), F32, kind="Internal").ap()
    ids_dram = nc.dram_tensor("ids_dram", (NSLOT * P, 1), F32, kind="Internal").ap()
    ys_dram = nc.dram_tensor("ys_dram", (NSLOT * P, H), F32, kind="Internal").ap()

    base = (nc.sbuf_base + 31) // 32 * 32
    end = nc.sbuf_usable_end
    ctx = ExitStack()
    arena = ctx.enter_context(nc.sbuf_tensor("arena", [P, (end - base) // 32 * 32 - 64], U8))
    cursor = {}

    def region(name, at):
        cursor[name] = [at, at]

    def sb(where, name, shape, dt):
        size = {F32: 4, F32R: 4, I32: 4, BF16: 2, U8: 1}[dt]
        for d in shape[1:]:
            size *= d
        t = nc.alloc_sbuf_tensor_at(name, shape, dt, offset=cursor[where][1])
        cursor[where][1] += (size + 31) // 32 * 32
        assert cursor[where][1] <= end, (name, cursor[where][1] - end)
        return t

    EXPERT_BYTES = E * (KC * 2 * M + MC * H) * 4
    WORK_BYTES, ROUTE_BYTES = 44 * 1024, 14 * 1024 + 512
    SHARED_BYTES = 2 * (KC * 2 * SM + SM // P * H) * 4
    region("experts", base)
    region("stage", base)
    region("shared", base + EXPERT_BYTES)
    region("work", base + EXPERT_BYTES + SHARED_BYTES)
    region("route", base + EXPERT_BYTES + SHARED_BYTES + WORK_BYTES)
    region("tiny", base + EXPERT_BYTES + SHARED_BYTES + WORK_BYTES + ROUTE_BYTES)
    region("attn_a", cursor["experts"][0])
    region("attn_w", cursor["shared"][0])
    region("attn_b", cursor["work"][0])
    region("attn_c", cursor["route"][0])

    wgu = sb("experts", "wgu", [P, E, KC, 2 * M], F32)
    wdn = sb("experts", "wdn", [P, E, MC, H], F32)
    raw = [sb("stage", f"raw{j}", [P, KC, SM], F32) for j in range(3)]
    sh_w = [[sb("shared", f"sw{j}{half}", [P, KC, SM], F32R) for half in "hl"] for j in range(3)]

    xb = sb("work", "xb", [P, 4, H], F32)
    xT0 = sb("work", "xT0", [P, 2, KC, P], F32)
    region("prep", cursor["work"][1])
    xTh = sb("work", "xTh", [P, 2, KC, P], F32R)
    xTl = sb("work", "xTl", [P, 2, KC, P], F32R)
    act_h = sb("work", "act_h", [P, 2, SM], F32)
    hTh = sb("work", "hTh", [P, KC, P], F32R)
    hTl = sb("work", "hTl", [P, KC, P], F32R)
    prep_end = cursor["work"][1]
    mixb = sb("work", "mixb", [P, 2, H], F32)
    eact = sb("work", "eact", [P, 2, M], F32)
    ehT = sb("work", "ehT", [P, 2, MC, P], F32)
    xe = sb("work", "xe", [P, 2, H], F32)

    ident = sb("tiny", "ident", [P, P], F32)
    below = sb("route", "below", [P, P], BF16)
    ones_b = sb("route", "ones_b", [P, P], BF16)
    ones_f = sb("route", "ones_f", [NB, P], F32)
    tok = sb("tiny", "tok", [P, NB], F32)
    rank8 = sb("route", "rank8", [P, E], F32)
    steps128 = sb("route", "steps128", [P, MAXT - 1], F32)
    slots = sb("route", "slots", [P, NSLOT], F32)
    zeros = sb("tiny", "zeros", [P, P], F32)
    wt_row = sb("route", "wt_row", [E, H], F32)
    wg_row = sb("route", "wg_row", [E, G], F32)
    cond_row = sb("route", "cond_row", [NB, G], F32)
    wtT = sb("route", "wtT", [P, KC, E], F32)
    wgT = sb("route", "wgT", [G, E], F32)
    condT = sb("route", "condT", [G, NB], F32)
    glog = sb("route", "glog", [NB, E], F32)
    gdiag = sb("route", "gdiag", [NB, NB, E], F32)
    r = {k: sb("route", "r_" + k, [P, NB, E], F32) for k in ("logit", "oh1", "oh2", "a", "b")}
    picks = sb("route", "picks", [P, NB, E], BF16)
    c = {k: sb("tiny", "c_" + k, [P, NB], F32) for k in ("max1", "max2", "t", "sum", "w1", "w2", "p")}
    small = {k: sb("route", "s_" + k, [P, E], F32) for k in ("n", "tiles", "ends", "base", "z")}
    many = sb("route", "many", [P, E, MAXT - 1], F32)
    per_slot = sb("route", "per_slot", [P, NSLOT, E - 1], F32)
    pos = sb("tiny", "pos", [P, NB, 2], I32)
    e_of_slot = sb("tiny", "e_of_slot", [P, 4 + NSLOT], I32)
    cur_pos = sb("tiny", "cur_pos", [P, 4, 2], I32)
    cur_tok = sb("tiny", "cur_tok", [P, 4, 1], F32)
    id_row = sb("tiny", "id_row", [NSLOT, P], F32)
    idx = sb("tiny", "idx", [P, NSLOT], I32)
    cur_idx = sb("tiny", "cur_idx", [P, 4, 1], I32)
    yb = mixb

    NH = null_bias.shape[0]
    D = G
    QC = NH * D // P
    KW = 2 * D + D + NH
    woh, wol = (sb("attn_a", f"wo_{half}", [P, QC, H], F32R) for half in "hl")
    qTh, qTl = (sb("attn_a", f"qT_{half}", [P, 2, QC, 2 * P], F32R) for half in "hl")
    xnh, xnl = (sb("attn_a", f"xnT_{half}", [P, 2, KC, 2 * P], F32R) for half in "hl")
    region("wo_raw", cursor["attn_a"][1])
    wo_raw = sb("wo_raw", "wo_raw", [P, QC, H], F32)
    pTh, pTl = (sb("attn_a", f"pT_{half}", [P, NH, P], F32R) for half in "hl")
    wqh, wql = (sb("attn_w", f"wq_{half}", [P, KC, NH * D], F32R) for half in "hl")
    wkh, wkl = (sb("attn_w", f"wk_{half}", [P, KC, KW], F32R) for half in "hl")
    region("wq_raw", cursor["attn_w"][1])
    wq_raw = sb("wq_raw", "wq_raw", [P, 2, NH * D], F32)
    vzh, vzl = (sb("attn_w", f"vz_{half}", [P, 4, 4, D], F32R) for half in "hl")
    x1 = sb("attn_b", "x1", [P, 2, H], F32)
    y1 = sb("attn_b", "y1", [P, 2, H], F32)
    y2 = sb("attn_b", "y2", [P, 2, H], F32)
    resid = sb("attn_b", "resid", [P, 2, H], F32)
    ob = sb("attn_b", "ob", [P, 2, H], F32)
    kzh, kzl = (sb("attn_b", f"kz_{half}", [P, 2, 2, 2, P], F32R) for half in "hl")
    oTh, oTl = (sb("attn_b", f"oT_{half}", [P, QC, P], F32R) for half in "hl")
    prob = sb("attn_b", "prob", [P, NH, P], F32)
    assert cursor["attn_a"][1] <= cursor["shared"][0] and cursor["attn_w"][1] <= cursor["work"][0]
    assert cursor["attn_b"][1] <= cursor["route"][0] and cursor["work"][1] <= cursor["route"][0]
    assert cursor["route"][1] <= cursor["tiny"][0], cursor
    bias = sb("attn_c", "bias", [P, NH, P], F32)
    null_tmp = sb("prep", "null_tmp", [P, NH * D], F32)
    gout = sb("attn_c", "gout", [P, H], F32)
    woxh, woxl = (sb("attn_c", f"wox_{half}", [P, H], F32R) for half in "hl")
    ident_b = sb("tiny", "ident_b", [P, P], BF16)
    mask_in = sb("prep", "mask_in", [NB, P // 4], I32)
    mneg = sb("tiny", "mneg", [P, P], BF16)
    gin = sb("prep", "gin", [P, KC], F32)
    gin8 = sb("prep", "gin8", [P, KC], F32)
    nkb = sb("prep", "nkb", [P, D], F32)
    nvc = sb("prep", "nvc", [P, 1], F32)
    nbb = sb("tiny", "nbb", [P, NH], F32)
    nvsel = sb("attn_c", "nvsel", [P, QC * NH], F32)
    wnull = sb("prep", "wnull", [P, KC, NH], F32)
    wkv_raw = sb("prep", "wkv_raw", [P, KC, 2 * D], F32)
    nln = sb("tiny", "nln", [P, 4, NH], F32)
    a16 = {k: sb("tiny", "a_" + k, [P, NH], F32) for k in ("max", "negm", "shift", "sum", "p0", "tot", "rs")}
    p0pad = sb("attn_w", "p0pad", [P, P], F32)
    p0Th, p0Tl = (sb("attn_w", f"p0T_{half}", [P, P], F32R) for half in "hl")
    ln = {k: sb("tiny", "ln_" + k, [P, n], F32) for k, n in (("st", 6), ("mv", 2), ("ve", 1), ("rs", 1))}
    fl = {k: sb("tiny", "fl_" + k, [P, n], F32) for k, n in (("st", 6), ("mv", 2), ("ve", 1), ("rs", 1))}
    half_neg = sb("tiny", "half_neg", [P, 1], F32)
    eps = sb("tiny", "eps", [P, 1], F32)
    spare = sb("tiny", "spare", [1, 6], F32)
    cur_y = sb("tiny", "cur_y", [P, 4, 2], I32)
    assert cursor["attn_c"][1] <= cursor["tiny"][0] and cursor["prep"][1] <= prep_end
    x1_dram = nc.dram_tensor("x1_dram", (NT, H), F32, kind="Internal").ap()

    ps = [ctx.enter_context(nc.psum_tensor(f"bank{j}", [P, 512], F32)) for j in range(8)]
    T_, H_, L_, D_ = ps[0], ps[1], ps[2], ps[3]
    GB, UB = ps[4:6], ps[6:8]

    names = {}

    def sem(name):
        names[name] = ctx.enter_context(nc.semaphore(name))
        return names[name]

    consts = sem("consts_written")
    small_in = sem("small_inputs_in")
    raw_in = [sem(f"shared_raw_in{j}") for j in range(3)]
    sh_hi, sh_lo = sem("shared_high_split"), sem("shared_low_split")
    prep_t, prep_c = sem("router_weights_turned"), sem("router_weights_copied")
    experts_in = sem("expert_weights_in")
    x_in = [sem(f"x_tile_in{s}") for s in range(4)]
    xe_in = [sem(f"late_tile_in{s}") for s in range(2)]
    et, ec, elg = sem("late_turned"), sem("late_copied"), sem("late_logits_done")
    raw_ok, lg = sem("early_xT_copied"), sem("early_logits_done")
    route_v, picks_ok, ranks_ok = sem("route_step"), sem("picks_ready"), sem("ranks_done")
    exp_ok, soft_ok = sem("route_exp_done"), sem("route_shift_ready")
    pos_ok = sem("positions_ready")
    ids_zero, ids_row_in, ids_T, idx_ok = sem("ids_cleared"), sem("ids_row_in"), sem("ids_turned"), sem("idx_ready")
    scat = [sem(f"scattered{s}") for s in range(4)]
    xt, xhi, xlo = sem("x_turned"), sem("xT_high"), sem("xT_low")
    gd, ud, dd = sem("gate_done"), sem("up_done"), sem("down_done")
    sg, lk, hd = sem("gate_scaled"), sem("leaky_done"), sem("hidden_done")
    ht, hhi, hlo = sem("h_turned"), sem("hT_high"), sem("hT_low")
    mixed = sem("mix_ready")
    mix_out = [sem(f"mix_stored{s}") for s in range(2)]
    gath = [sem(f"gathered{s}") for s in range(4)]
    ext, exc = sem("e_x_turned"), sem("e_xT_copied")
    egu, esg, elk, ehd = sem("e_gate_up_done"), sem("e_gate_scaled"), sem("e_leaky_done"), sem("e_hidden_done")
    eht, ehc, edn, eyc = sem("e_h_turned"), sem("e_hT_copied"), sem("e_down_done"), sem("e_y_copied")
    ys_out = [sem(f"ys_stored{s}") for s in range(2)]

    N_FILLS, N_CONST = 5, 11
    N_SMALL = 3

    a_small, bias_in, wq_in, wo_in = sem("attn_small_in"), sem("bias_in"), [sem("wq_in0"), sem("wq_in1")], sem("wo_in")
    a_const, g8_ok = sem("attn_consts"), sem("gain_scaled")
    wq_hi, wq_lo = sem("wq_high"), sem("wq_low")
    null_s, wn_ok = sem("null_step"), sem("null_weights_ready")
    wk_hi, wk_lo = sem("wk_high"), sem("wk_low")
    nvs_ok, nvw_done, wox_hi, wox_lo = sem("null_value_select"), sem("null_value_done"), sem("wox_high"), sem("wox_low")
    wo_hi, wo_lo = sem("wo_high"), sem("wo_low")
    z_in, x1_out = [sem(f"mix_in{j}") for j in range(2)], [sem(f"x1_stored{j}") for j in range(2)]
    y_in = [sem(f"y_gathered{j}") for j in range(2)]
    rb_in, o_out = [sem(f"resid_in{j}") for j in range(2)], [sem(f"out_stored{j}") for j in range(2)]
    ln_s, ln_ve, ln_rs, xn_ok = sem("norm_in_step"), sem("norm_in_eps"), sem("norm_in_scale"), sem("xn_ready")
    pj, pj_hi, pj_lo = sem("proj_done"), sem("proj_high"), sem("proj_low")
    sim_d, ttr_d = sem("scores_done"), sem("biased_scores_done")
    neg_ok, shift_ok, exp_d = sem("row_max_ready"), sem("null_shift_ready"), sem("exp_done")
    tot_ok, rs_ok, p0_ok, norm_ok = sem("sum_ready"), sem("sum_inverse_ready"), sem("null_prob_ready"), sem("probs_normal")
    pt_d, pt_hi, pt_lo = sem("probs_turned"), sem("probsT_high"), sem("probsT_low")
    pv_d, pv_hi, pv_lo = sem("pv_done"), sem("pv_high"), sem("pv_low")
    wo_d, f_s, f_ve, f_rs, f_n = sem("out_proj_done"), sem("norm_out_step"), sem("norm_out_eps"), sem("norm_out_scale"), sem("norm_out_done")
    f_g, f_o = sem("out_gained"), sem("out_ready")
    block = ctx.enter_context(nc.Block())

    def at(i, s, d):
        return i + (s + d) // 4, (s + d) % 4

    def exists(i, s):
        return not isinstance(i, int) or 0 <= 4 * i + s < NB

    FIRST = 10
    ORDER = (("x", "v", "k", "q0", "q1", "p0"), ("x", "v", "q2", "q3", "p0"))

    def event(i, s, what):
        if not (isinstance(i, int) and i == NB // 4 - 1):
            return FIRST + 22 * i + 11 * (s // 2) + (6 if s % 2 else 0) + ORDER[s % 2].index(what)
        ahead = {"x": 3, "p0": 0}
        done = [(t, w) for t in range(4) for w in ORDER[t % 2] if 4 * i + t + ahead.get(w, 2) < NB]
        return FIRST + 22 * i + done.index((s, what))

    def bank_of(i, s, what):
        return event(i if isinstance(i, int) else 0, s, what) % 2

    def wait_apart(eng, sem, count, word):
        eng.wait_ge(sem, count)
        eng.memset(spare[:, word:word + 1], 0.0)

    N_ASMALL = 7

    def attention_sync(sp):
        sp.wait_ge(edn, NSLOT)
        sp.wait_ge(null_s, 2 * KC)
        sp.wait_ge(wk_lo, KC)
        sp.dma_start(gout[:], g_out.rearrange("(a h) -> a h", a=1).to_broadcast([P, H])).then_inc(wo_in, 16)

        def load_mix(i, s):
            b, par = 4 * i + s, s % 2
            if not exists(i, s):
                return
            since(sp, xn_ok, b - 1)
            since(sp, x1_out[par], 16 * (2 * i + s // 2))
            sp.dma_start(x1[:, par, :], mix_dram[bass.ts(b, P), :]).then_inc(z_in[par], 16)

        def store_x1(i, s):
            b, par = 4 * i + s, s % 2
            if not exists(i, s):
                return
            sp.wait_ge(ln_s, 4 * b + 2)
            sp.dma_start(x1_dram[bass.ts(b, P), :], x1[:, par, :]).then_inc(x1_out[par], 16)

        def load_resid(i, s):
            b, par = 4 * i + s, s % 2
            since(sp, f_o, b - 1)
            sp.wait_ge(x1_out[par], 16 * (2 * i + s // 2 + 1))
            sp.dma_start(resid[:, par, :], x1_dram[bass.ts(b, P), :]).then_inc(rb_in[par], 16)

        def store_out(i, s):
            b, par = 4 * i + s, s % 2
            if not exists(i, s):
                return
            sp.wait_ge(f_o, b + 1)
            sp.dma_start(out[bass.ds(b, 1)].rearrange("a s h -> (a s) h"), ob[:, par, :]).then_inc(o_out[par], 16)

        load_mix(0, 0)
        load_mix(0, 1)
        for j in range(2):
            sp.wait_ge(y_in[j], 32)
        sp.dma_start(wo_raw[:], wo.rearrange("(c p) n -> p c n", p=P)).then_inc(wo_in, 16)
        for s in range(2):
            store_x1(0, s)
            load_mix(0, s + 2)
        for s in range(2, 4):
            store_x1(0, s)

        def slot(i, s):
            load_mix(*at(i, s, 4))
            load_resid(i, s)
            store_x1(*at(i, s, 4))
            store_out(*at(i, s, -1))

        quads(sp, NB, slot)
        store_out(NB // 4 - 1, 3)
        for j in range(2):
            sp.wait_ge(o_out[j], 16 * (NB // 2))

    def attention_gpsimd(pl):
        pl.wait_ge(bias_in, 16)
        pl.affine_select(out=bias[:], in_=bias[:], compare_op=ALU.is_ge, fill=NEG, base=0,
                         pattern=[[0, NH], [-1, P]], channel_multiplier=1).then_inc(a_const, 1)
        pl.memset(half_neg[:], -0.5).then_inc(a_const, 1)
        pl.memset(eps[:], EPS).then_inc(a_const, 1)
        pl.tensor_copy(ident_b[:], ident[:]).then_inc(a_const, 1)
        pl.wait_ge(wq_lo, KC)
        pl.wait_ge(wk_lo, KC)
        pl.wait_ge(null_s, 2 * KC)
        for z in (vzh, vzl, woxh, woxl, p0pad):
            pl.memset(z[:].bitcast(F32), 0.0).then_inc(a_const, 1)
        pl.tensor_copy(cur_y[:], pos[:, 0:4, :])
        pl.drain()
        pl.wait_ge(edn, NSLOT)
        pl.wait_ge(eyc, NSLOT)
        for j in range(2):
            pl.wait_ge(ys_out[j], 16 * (NSLOT // 2))

        def gather(i, s):
            b, par = 4 * i + s, s % 2
            if not exists(i, s):
                return
            if isinstance(b, int) and b >= 2 or not isinstance(b, int):
                if isinstance(i, int) and i == 0:
                    pl.wait_ge(pj, 1 + (b - 2))
                elif isinstance(i, int) and i == 1 and s == 0:
                    pl.wait_ge(pj, FIRST)
                else:
                    pl.wait_ge(pj, event(*at(i, s, -5), "x") + 1)
            if not (isinstance(i, int) and i == 0):
                pl.tensor_copy(cur_y[:, s, :], pos[:, bass.ds(b, 1), :].rearrange("p a b -> p (a b)"))
                pl.drain()
            for k, y in enumerate((y1, y2)):
                pl.indirect_dma_start(y[:, par, :], None, ys_dram,
                                      bass.IndirectOffsetOnAxis(ap=cur_y[:, s, k:k + 1], axis=0)).then_inc(y_in[par], 16)

        def scale_in(i, s):
            b = 4 * i + s
            if not exists(i, s):
                return
            pl.wait_ge(ln_s, 4 * b + 4)
            pl.tensor_tensor(ln["ve"][:], ln["mv"][:, 1:2], eps[:], ALU.add).then_inc(ln_ve, 1)
            pl.wait_ge(ln_ve, b + 1)
            pl.tensor_tensor(ln["rs"][:], ln["ve"][:], half_neg[:], ALU.pow).then_inc(ln_rs, 1)

        def normal(i, s, hf):
            b = 4 * i + s
            pl.wait_ge(rs_ok, 2 * b + hf + 1)
            hs = slice(hf * NH // 2, (hf + 1) * NH // 2)
            pl.tensor_tensor(prob[:, hs, :], prob[:, hs, :],
                             a16["rs"][:, hs].unsqueeze(2).to_broadcast([P, NH // 2, P]), ALU.mult).then_inc(norm_ok, 1)

        def finish(i, s):
            b, par = 4 * i + s, s % 2
            if not exists(i, s):
                return
            pl.wait_ge(f_s, 2 * b + 2)
            pl.tensor_tensor(fl["ve"][:], fl["mv"][:, 1:2], eps[:], ALU.add).then_inc(f_ve, 1)
            pl.wait_ge(f_ve, b + 1)
            pl.tensor_tensor(fl["rs"][:], fl["ve"][:], half_neg[:], ALU.pow).then_inc(f_rs, 1)
            pl.wait_ge(f_n, b + 1)
            pl.tensor_tensor(ob[:, par, :], ob[:, par, :], gout[:], ALU.mult).then_inc(f_g, 1)
            pl.wait_ge(f_g, b + 1)
            pl.wait_ge(rb_in[par], 8 * (b - par) + 16)
            pl.tensor_tensor(ob[:, par, :], ob[:, par, :], resid[:, par, :], ALU.add).then_inc(f_o, 1)

        for s in range(2):
            gather(0, s)
        for z in (kzh, kzl):
            pl.memset(z[:].bitcast(F32), 0.0).then_inc(a_const, 1)
        pl.wait_ge(a_const, 11)
        for s in range(4):
            scale_in(0, s)
            if s < 2:
                gather(0, s + 2)

        def slot(i, s):
            gather(*at(i, s, 4))
            normal(i, s, 0)
            scale_in(*at(i, s, 4))
            normal(i, s, 1)
            finish(*at(i, s, -1))

        quads(pl, NB, slot)
        finish(NB // 4 - 1, 3)

    def wq_high(act, k):
        if k == 0:
            act.wait_ge(dd, NB)
        act.wait_ge(g8_ok, 1)
        act.wait_ge(wq_in[k % 2], 16 * (k // 2 + 1))
        act.activation(wqh[:, k, :], wq_raw[:, k % 2, :], ACT.Copy, scale=gin8[:, k:k + 1]).then_inc(wq_hi, 1)
        act.activation(wkh[:, k, 0:2 * D].rearrange("p (a d) -> p a d", a=2),
                       wkv_raw[:, k, 0:D].unsqueeze(1).to_broadcast([P, 2, D]), ACT.Copy, scale=gin[:, k:k + 1])
        act.activation(wkh[:, k, 2 * D:3 * D], wkv_raw[:, k, D:2 * D], ACT.Copy, scale=gin[:, k:k + 1])
        act.wait_ge(null_s, 2 * k + 2)
        act.activation(wkh[:, k, 3 * D:KW], wnull[:, k, :], ACT.Copy).then_inc(wk_hi, 1)

    def wq_low(dve, k):
        if k == 0:
            dve.wait_ge(a_small, 16 * N_ASMALL)
            dve.wait_ge(dd, NB)
            dve.tensor_scalar(gin8[:], gin[:], float(D) ** -0.5, None, ALU.mult).then_inc(g8_ok, 1)
            dve.memset(mneg[:], 0.0).then_inc(g8_ok, 1)
            dve.memset(nvsel[:], 0.0).then_inc(g8_ok, 1)
            dve.wait_ge(g8_ok, 3)
            dve.tensor_scalar(mneg[0:NB, :], mask_in[:].bitcast(U8), -1.0, -NEG, ALU.add, ALU.mult).then_inc(g8_ok, 1)
            for j in range(2):
                ins = dve.tensor_copy(nvsel[j * D:(j + 1) * D, j::NH + 2],
                                      nvc[j * D:(j + 1) * D, :].to_broadcast([D, QC]))
            ins.then_inc(nvs_ok, 1)
        dve.wait_ge(wq_in[k % 2], 16 * (k // 2 + 1))
        since(dve, null_s, 2 * k)
        dve.scalar_tensor_tensor(null_tmp[:].rearrange("p (h d) -> p h d", d=D),
                                 wq_raw[:, k % 2, :].rearrange("p (h d) -> p h d", d=D), gin8[:, k:k + 1],
                                 nkb[:].unsqueeze(1).to_broadcast([P, NH, D]), ALU.mult, ALU.mult).then_inc(null_s, 1)
        dve.wait_ge(null_s, 2 * k + 1)
        dve.tensor_reduce(wnull[:, k, :], null_tmp[:].rearrange("p (h d) -> p h d", d=D), AX.X, ALU.add).then_inc(null_s, 1)
        dve.wait_ge(wq_hi, k + 1)
        dve.scalar_tensor_tensor(wql[:, k, :], wq_raw[:, k % 2, :], gin8[:, k:k + 1], wqh[:, k, :].bitcast(F32),
                                 ALU.mult, ALU.subtract).then_inc(wq_lo, 1)
        dve.wait_ge(wk_hi, k + 1)
        dve.scalar_tensor_tensor(wkl[:, k, 0:2 * D].rearrange("p (a d) -> p a d", a=2),
                                 wkv_raw[:, k, 0:D].unsqueeze(1).to_broadcast([P, 2, D]), gin[:, k:k + 1],
                                 wkh[:, k, 0:2 * D].bitcast(F32).rearrange("p (a d) -> p a d", a=2),
                                 ALU.mult, ALU.subtract)
        dve.scalar_tensor_tensor(wkl[:, k, 2 * D:3 * D], wkv_raw[:, k, D:2 * D], gin[:, k:k + 1],
                                 wkh[:, k, 2 * D:3 * D].bitcast(F32), ALU.mult, ALU.subtract)
        dve.tensor_tensor(wkl[:, k, 3 * D:KW], wnull[:, k, :], wkh[:, k, 3 * D:KW].bitcast(F32),
                          ALU.subtract).then_inc(wk_lo, 1)

    SB = ps[0:4]
    OB = ps[4:6]
    AB = ps[6:8]

    def halves(engine, kind, dst_h, dst_l, src):
        if kind == "h":
            return engine.activation(dst_h, src, ACT.Copy)
        return engine.tensor_tensor(dst_l, src, dst_h.bitcast(F32), ALU.subtract)

    def evacuate(eng, kind):
        mine, done = (pj_hi, pj) if kind == "h" else (pj_lo, pj_hi)

        def bank(m, par):
            eng.wait_ge(done, m + 1)
            return AB[par]

        def x(i, s, m, par):
            q, j = (s // 2) % 2, s % 2
            src = bank(m, par)[:].rearrange("p (k n) -> p k n", k=KC)
            cols = slice(j * P, (j + 1) * P)
            halves(eng, kind, xnh[:, q, :, cols], xnl[:, q, :, cols], src).then_inc(mine, 1)

        def v(i, s, m, par):
            src = bank(m, par)
            vs = src[:, 0:D].unsqueeze(1).to_broadcast([P, 2, D])
            ins = halves(eng, kind, vzh[:, s, 0:4:3, :], vzl[:, s, 0:4:3, :], vs)
            if kind == "l":
                ins = eng.scalar_tensor_tensor(nln[:, s, :], src[:, D:D + NH], -1.0, nbb[:], ALU.mult, ALU.subtract)
            ins.then_inc(mine, 1)

        def k(i, s, m, par):
            src, q = bank(m, par), (s // 2) % 2
            for j in range(2):
                rows = slice(j * D, (j + 1) * D)
                ins = halves(eng, kind, kzh[rows, q, :, j, :], kzl[rows, q, :, j, :],
                             src[rows, 0:2 * P].rearrange("p (b n) -> p b n", b=2))
            ins.then_inc(mine, 1)

        def q(i, s, m, par, c):
            src, pr = bank(m, par), (s // 2) % 2
            halves(eng, kind, qTh[:, pr, 2 * c:2 * c + 2, :], qTl[:, pr, 2 * c:2 * c + 2, :],
                   src[:].rearrange("p (c n) -> p c n", c=2)).then_inc(mine, 1)

        def p0(i, s, m, par):
            halves(eng, kind, p0Th[:], p0Tl[:], bank(m, par)[:, 0:P]).then_inc(mine, 1)

        return x, v, k, q, p0

    def attention_scalar(act):
        act.wait_ge(edn, NSLOT)
        act.wait_ge(a_const, 11)
        x, v, k, q, p0 = evacuate(act, "h")

        def exps(i, s, hf, halfway=lambda: None):
            b = 4 * i + s
            act.wait_ge(shift_ok, 2 * b + hf + 1)
            for h in range(hf * NH // 2, (hf + 1) * NH // 2):
                if h % (NH // 2) == NH // 4:
                    halfway()
                act.activation(prob[:, h, :], prob[:, h, :], ACT.Exp, bias=a16["negm"][:, h:h + 1],
                               accum_out=a16["sum"][:, h:h + 1])
            hs = slice(hf * NH // 2, (hf + 1) * NH // 2)
            act.activation(a16["p0"][:, hs], a16["shift"][:, hs], ACT.Exp).then_inc(exp_d, 1)

        def pv(i, s):
            b = 4 * i + s
            if not exists(i, s):
                return
            for m in range(2):
                act.wait_ge(pv_d, 2 * b + m + 1)
                if m == 0:
                    since(act, wo_d, b)
                cs = slice(m * QC // 2, (m + 1) * QC // 2)
                act.activation(oTh[:, cs, :], OB[m][:].rearrange("p (c n) -> p c n", c=QC // 2), ACT.Copy).then_inc(pv_hi, 1)

        def turned(i, s):
            b = 4 * i + s
            for n in range(4):
                act.wait_ge(pt_d, 4 * b + n + 1)
                since(act, pv_d, 2 * b)
                act.activation(pTh[:, 4 * n:4 * n + 4, :], SB[n][:].rearrange("p (h n) -> p h n", h=4), ACT.Copy).then_inc(pt_hi, 1)


        def split_wo(n):
            if n < 3:
                return
            act.wait_ge(wo_in, 32)
            cs = slice(2 * (n - 3), 2 * (n - 2))
            act.activation(woh[:, cs, :], wo_raw[:, cs, :], ACT.Copy).then_inc(wo_hi, 1)

        first(x, v, k, q, split_wo)
        act.wait_ge(nvw_done, 1)
        act.activation(woxh[0:NH, :], SB[0][0:NH, :], ACT.Copy).then_inc(wox_hi, 1)

        def slot(i, s):
            projections(i, s, "x", x=x)
            exps(i, s, 0)
            projections(i, s, "v", v=v)
            pv(*at(i, s, -1))
            exps(i, s, 1, lambda: projections(i, s, "k", k=k))
            projections(i, s, "q", q=q)
            turned(i, s)
            p0(i, s, event(i, s, "p0"), bank_of(i, s, "p0"))

        quads(act, NB, slot)
        pv(NB // 4 - 1, 3)

    def first(x, v, k, q, between=None):
        for b in range(2):
            x(0, b, b, b % 2)
        for b in range(2):
            v(0, b, 2 + b, b % 2)
            if between:
                between(b)
        k(0, 0, 4, 0)
        if between:
            between(2)
        for c in range(4):
            q(0, 0, 5 + c, (5 + c) % 2, c)
            if between:
                between(3 + c)
        x(0, 2, 9, 1)

    def projections(i, s, which, **make):
        for what in ORDER[s % 2]:
            kind = what[0]
            ahead = at(i, s, 3 if kind == "x" else 2)
            if kind not in which or not exists(*ahead):
                continue
            place = (event(i, s, what), bank_of(i, s, what))
            if kind == "q":
                make["q"](*ahead, *place, int(what[1]))
            else:
                make[kind](*ahead, *place)

    def attention_vector(dve):
        dve.wait_ge(edn, NSLOT)
        x, v, k, q, p0 = evacuate(dve, "l")

        def norm_in(i, s):
            b, par = 4 * i + s, s % 2
            if not exists(i, s):
                return
            dve.wait_ge(z_in[par], 8 * (b - par) + 16)
            dve.wait_ge(y_in[par], 16 * (b - par) + 32)
            dve.scalar_tensor_tensor(x1[:, par, :], y1[:, par, :], c["w1"][:, bass.ds(b, 1)], x1[:, par, :],
                                     ALU.mult, ALU.add).then_inc(ln_s, 1)
            dve.wait_ge(ln_s, 4 * b + 1)
            dve.scalar_tensor_tensor(x1[:, par, :], y2[:, par, :], c["w2"][:, bass.ds(b, 1)], x1[:, par, :],
                                     ALU.mult, ALU.add).then_inc(ln_s, 1)
            dve.wait_ge(ln_s, 4 * b + 2)
            dve.bn_stats(ln["st"][:], x1[:, par, :]).then_inc(ln_s, 1)
            wait_apart(dve, ln_s, 4 * b + 3, 5)
            dve.bn_aggr(ln["mv"][:], ln["st"][:]).then_inc(ln_s, 1)

        def norm_apply(i, s):
            b, par = 4 * i + s, s % 2
            if not exists(i, s):
                return
            dve.wait_ge(ln_rs, b + 1)
            dve.tensor_scalar(y1[:, par, :], x1[:, par, :], ln["mv"][:, 0:1], ln["rs"][:, 0:1],
                              ALU.subtract, ALU.mult).then_inc(xn_ok, 1)

        def scores(i, s, hf):
            b = 4 * i + s
            if hf == 0:
                since(dve, pt_d, 4 * b)
            for h in range(hf * NH // 2, (hf + 1) * NH // 2):
                if h % 4 == 0:
                    wait_apart(dve, sim_d, 4 * b + h // 4 + 1, h // 4)
                ins = dve.tensor_tensor_reduce(prob[:, h, :], SB[h // 4][:, (h % 4) * P:(h % 4 + 1) * P], bias[:, h, :],
                                               1.0, -3.0e38, ALU.add, ALU.max, a16["max"][:, h:h + 1])
            ins.then_inc(ttr_d, 1)
            hs = slice(hf * NH // 2, (hf + 1) * NH // 2)
            dve.wait_ge(ttr_d, 2 * b + hf + 1)
            dve.scalar_tensor_tensor(a16["negm"][:, hs], a16["max"][:, hs], -1.0, nln[:, s, hs],
                                     ALU.mult, ALU.min).then_inc(neg_ok, 1)
            dve.wait_ge(neg_ok, 2 * b + hf + 1)
            dve.tensor_tensor(a16["shift"][:, hs], a16["negm"][:, hs], nln[:, s, hs], ALU.subtract).then_inc(shift_ok, 1)

        def sums(i, s, hf):
            b = 4 * i + s
            hs = slice(hf * NH // 2, (hf + 1) * NH // 2)
            dve.wait_ge(exp_d, 2 * b + hf + 1)
            dve.tensor_tensor(a16["tot"][:, hs], a16["sum"][:, hs], a16["p0"][:, hs], ALU.add).then_inc(tot_ok, 1)
            dve.wait_ge(tot_ok, 2 * b + hf + 1)
            dve.reciprocal(a16["rs"][:, hs], a16["tot"][:, hs]).then_inc(rs_ok, 1)
            dve.wait_ge(rs_ok, 2 * b + hf + 1)
            dve.tensor_tensor(p0pad[:, hs], a16["p0"][:, hs], a16["rs"][:, hs], ALU.mult).then_inc(p0_ok, 1)

        def pv(i, s):
            b = 4 * i + s
            if not exists(i, s):
                return
            for m in range(2):
                dve.wait_ge(pv_hi, 2 * b + m + 1)
                cs = slice(m * QC // 2, (m + 1) * QC // 2)
                halves(dve, "l", oTh[:, cs, :], oTl[:, cs, :],
                       OB[m][:].rearrange("p (c n) -> p c n", c=QC // 2)).then_inc(pv_lo, 1)

        def out_stats(i, s):
            b = 4 * i + s
            if not exists(i, s):
                return
            dve.wait_ge(wo_d, b + 1)
            dve.bn_stats(fl["st"][:], OB[0][:]).then_inc(f_s, 1)
            wait_apart(dve, f_s, 2 * b + 1, 4)
            dve.bn_aggr(fl["mv"][:], fl["st"][:]).then_inc(f_s, 1)

        def out_norm(i, s):
            b, par = 4 * i + s, s % 2
            if not exists(i, s):
                return
            dve.wait_ge(f_rs, b + 1)
            since(dve, o_out[par], 8 * (b - par))
            dve.tensor_scalar(ob[:, par, :], OB[0][:], fl["mv"][:, 0:1], fl["rs"][:, 0:1],
                              ALU.subtract, ALU.mult).then_inc(f_n, 1)

        def turned(i, s, n):
            b = 4 * i + s
            dve.wait_ge(pt_hi, 4 * b + n + 1)
            halves(dve, "l", pTh[:, 4 * n:4 * n + 4, :], pTl[:, 4 * n:4 * n + 4, :],
                   SB[n][:].rearrange("p (h n) -> p h n", h=4)).then_inc(pt_lo, 1)

        for s in range(2):
            norm_in(0, s)
            norm_apply(0, s)
        dve.wait_ge(a_const, 11)

        def between(n):
            if n < 4:
                (norm_apply if n % 2 else norm_in)(0, 2 + n // 2)
            if n >= 3:
                dve.wait_ge(wo_hi, n - 2)
                cs = slice(2 * (n - 3), 2 * (n - 2))
                dve.tensor_tensor(wol[:, cs, :], wo_raw[:, cs, :], woh[:, cs, :].bitcast(F32),
                                  ALU.subtract).then_inc(wo_lo, 1)

        first(x, v, k, q, between)
        dve.wait_ge(wox_hi, 1)
        dve.tensor_tensor(woxl[0:NH, :], SB[0][0:NH, :], woxh[0:NH, :].bitcast(F32), ALU.subtract).then_inc(wox_lo, 1)

        def slot(i, s):
            scores(i, s, 0)
            projections(i, s, "x", x=x)
            scores(i, s, 1)
            sums(i, s, 0)
            projections(i, s, "v", v=v)
            pv(*at(i, s, -1))
            projections(i, s, "k", k=k)
            norm_in(*at(i, s, 4))
            sums(i, s, 1)
            projections(i, s, "q", q=q)
            norm_apply(*at(i, s, 4))
            out_stats(*at(i, s, -1))
            turned(i, s, 0)
            turned(i, s, 1)
            out_norm(*at(i, s, -1))
            turned(i, s, 2)
            turned(i, s, 3)
            p0(i, s, event(i, s, "p0"), bank_of(i, s, "p0"))

        quads(dve, NB, slot)
        pv(NB // 4 - 1, 3)
        out_stats(NB // 4 - 1, 3)
        out_norm(NB // 4 - 1, 3)

    def attention_tensor(pe):
        def bank(m, par):
            since(pe, pj_lo, m - 1)
            return AB[par]

        def x(i, s, m, par):
            b, j = 4 * i + s, s % 2
            dst = bank(m, par)
            pe.wait_ge(xn_ok, b + 1)
            for kk in range(KC):
                mm = pe.transpose(dst[:, kk * P:(kk + 1) * P], y1[:, j, kk * P:(kk + 1) * P], ident[:])
            mm.then_inc(pj, 1)

        def v(i, s, m, par):
            q_, cols = (s // 2) % 2, slice((s % 2) * P, (s % 2 + 1) * P)
            dst = bank(m, par)
            pe.wait_ge(pj_lo, m - 1 if isinstance(m, int) and m < FIRST else m)
            for kk in range(KC):
                mm = split3(pe, dst[:, 0:D + NH], (xnh[:, q_, kk, cols], xnl[:, q_, kk, cols]),
                            (wkh[:, kk, 2 * D:KW], wkl[:, kk, 2 * D:KW]), kk == 0, kk == KC - 1)
            mm.then_inc(pj, 1)

        def columns(dst, w, q_):
            for kk in range(KC):
                mm = split3(pe, dst, (w[0][:, kk, :], w[1][:, kk, :]), (xnh[:, q_, kk, :], xnl[:, q_, kk, :]),
                            kk == 0, kk == KC - 1)
            return mm

        def k(i, s, m, par):
            dst = bank(m, par)
            columns(dst[:, 0:2 * P], (wkh[:, :, 0:2 * D], wkl[:, :, 0:2 * D]), (s // 2) % 2).then_inc(pj, 1)

        def q(i, s, m, par, cc):
            dst = bank(m, par)
            for j in range(2):
                cols = slice((2 * cc + j) * P, (2 * cc + j + 1) * P)
                mm = columns(dst[:, j * 2 * P:(j + 1) * 2 * P], (wqh[:, :, cols], wql[:, :, cols]), (s // 2) % 2)
            mm.then_inc(pj, 1)

        def scores(i, s):
            b, q_, j = 4 * i + s, (s // 2) % 2, s % 2
            cols = slice(j * P, (j + 1) * P)
            if s % 2 == 0:
                if isinstance(i, int) and i == 0 and s == 0:
                    pe.wait_ge(pj_lo, FIRST)
                    pe.wait_ge(wox_lo, 1)
                else:
                    pe.wait_ge(pj_lo, event(*at(i, s, -1), "q3") + 1)
            for n in range(4):
                since(pe, pt_lo, 4 * b - 3 + n)
                pe.matmul(SB[n][:], ident_b[:, bass.ds(b, 1)].to_broadcast([P, P]),
                          mneg[:].unsqueeze(1).to_broadcast([P, 4, P]), start=True, stop=False)
                for cc in (2 * n, 2 * n + 1):
                    mm = split3(pe, SB[n][:, (cc % 2) * 2 * P:(cc % 2 + 1) * 2 * P],
                                (qTh[:, q_, cc, cols], qTl[:, q_, cc, cols]),
                                (kzh[:, q_, j].rearrange("p a n -> p (a n)"), kzl[:, q_, j].rearrange("p a n -> p (a n)")),
                                False, cc % 2 == 1)
                mm.then_inc(sim_d, 1)

        def turn_probs(i, s):
            b = 4 * i + s
            for n in range(4):
                if n % 2 == 0:
                    pe.wait_ge(norm_ok, 2 * b + n // 2 + 1)
                for h in range(4 * n, 4 * n + 4):
                    mm = pe.transpose(SB[n][:, (h % 4) * P:(h % 4 + 1) * P], prob[:, h, :], ident[:])
                mm.then_inc(pt_d, 1)
            m, par = event(i, s, "p0"), bank_of(i, s, "p0")
            dst = bank(m, par)
            pe.wait_ge(p0_ok, 2 * b + 2)
            pe.transpose(dst[:, 0:P], p0pad[:], ident[:]).then_inc(pj, 1)

        def pv(i, s):
            b = 4 * i + s
            if not exists(i, s):
                return
            for m in range(2):
                since(pe, pv_lo, 2 * b - 1 + m)
                if m == 0:
                    since(pe, f_n, b)
                pe.wait_ge(pt_lo, 4 * b + 2 * m + 2)
                for j in range(2):
                    hs = slice(8 * m + j, 8 * m + 8, 2)
                    mm = split3(pe, OB[m][:], (vzh[:, s, 2 * j:2 * j + 2, :].rearrange("p a d -> p (a d)"),
                                               vzl[:, s, 2 * j:2 * j + 2, :].rearrange("p a d -> p (a d)")),
                                (pTh[:, hs, :], pTl[:, hs, :]), j == 0, j == 1)
                mm.then_inc(pv_d, 1)

        def out_projection(i, s):
            b = 4 * i + s
            if not exists(i, s):
                return
            pe.wait_ge(pv_lo, 2 * b + 2)
            if isinstance(i, int) and i == 0 and s == 0:
                pe.wait_ge(wo_lo, 4)
                pe.wait_ge(wox_lo, 1)
            pe.wait_ge(pj_lo, event(i, s, "p0") + 1)
            for cc in range(QC):
                split3(pe, OB[0][:], (oTh[:, cc, :], oTl[:, cc, :]), (woh[:, cc, :], wol[:, cc, :]), cc == 0, False)
            split3(pe, OB[0][:], (p0Th[:], p0Tl[:]), (woxh[:], woxl[:]), False, True).then_inc(wo_d, 1)

        pe.wait_ge(wq_lo, KC)
        pe.wait_ge(wk_lo, KC)
        pe.wait_ge(g8_ok, 4)
        first(x, v, k, q)
        pe.wait_ge(wo_in, 32)
        pe.wait_ge(nvs_ok, 1)
        for cc in range(QC):
            mm = pe.matmul(SB[0][0:NH, :], nvsel[:, cc * NH:(cc + 1) * NH], wo_raw[:, cc, :],
                           start=(cc == 0), stop=(cc == QC - 1))
        mm.then_inc(nvw_done, 1)

        def slot(i, s):
            scores(i, s)
            projections(i, s, "x", x=x)
            pv(*at(i, s, -1))
            projections(i, s, "vkq", v=v, k=k, q=q)
            out_projection(*at(i, s, -1))
            turn_probs(i, s)

        quads(pe, NB, slot)
        pv(NB // 4 - 1, 3)
        out_projection(NB // 4 - 1, 3)

    def shared_steps(eng, step, after=lambda t: None):
        for s in range(4):
            step(0, s, True)
        with eng.Fori(1, EARLY // 4) as i:
            for s in range(4):
                step(i, s, True)
        for s in range(4):
            step(EARLY // 4, s, False)
            after(EARLY + s)
        with eng.Fori(EARLY // 4 + 1, NB // 4 - 1) as i:
            for s in range(4):
                step(i, s, False)
        for s in range(4):
            step(NB // 4 - 1, s, False)
            after(NB - 4 + s)

    @block.gpsimd
    def _(pl):
        pl.memset(ident[:], 0.0).then_inc(consts, 1)
        pl.memset(below[:], 1.0).then_inc(consts, 1)
        pl.memset(ones_b[:], 1.0).then_inc(consts, 1)
        pl.memset(ones_f[:], 1.0).then_inc(consts, 1)
        pl.memset(zeros[:], 0.0).then_inc(consts, 1)
        pl.wait_ge(consts, N_FILLS)
        pl.affine_select(out=ident[:], in_=ident[:], compare_op=ALU.not_equal, fill=1.0, base=0,
                         pattern=[[-1, P]], channel_multiplier=1).then_inc(consts, 1)
        pl.affine_select(out=below[:], in_=below[:], compare_op=ALU.is_gt, fill=0.0, base=0,
                         pattern=[[1, P]], channel_multiplier=-1).then_inc(consts, 1)
        exact = dict(allow_small_or_imprecise_dtypes=True)
        pl.iota(tok[:], pattern=[[P, NB]], base=0, channel_multiplier=1, **exact).then_inc(consts, 1)
        pl.iota(rank8[:], pattern=[[-1, E]], base=E, channel_multiplier=0, **exact).then_inc(consts, 1)
        pl.iota(steps128[:], pattern=[[P, MAXT - 1]], base=P, channel_multiplier=0, **exact).then_inc(consts, 1)
        pl.iota(slots[:], pattern=[[1, NSLOT]], base=0, channel_multiplier=0, **exact).then_inc(consts, 1)
        pl.wait_ge(pos_ok, 1)
        pl.wait_ge(ids_zero, 16)

        def scatter(i, s):
            if s == 0:
                for q in range(4):
                    since(pl, scat[q], 32 * i)
                pl.tensor_copy(cur_pos[:], pos[:, bass.ds(4 * i, 4), :])
                pl.tensor_copy(cur_tok[:].rearrange("p a b -> p (a b)"), tok[:, bass.ds(4 * i, 4)])
                pl.drain()
            for k in range(2):
                pl.indirect_dma_start(ids_dram, bass.IndirectOffsetOnAxis(ap=cur_pos[:, s, k:k + 1], axis=0),
                                      cur_tok[:, s, :], None).then_inc(scat[s], 16)

        quads(pl, NB, scatter)

        pl.wait_ge(idx_ok, 1)

        def gather(i, s):
            n = 4 * i + s
            if s == 0:
                for q in range(4):
                    since(pl, gath[q], 16 * i)
                pl.tensor_copy(cur_idx[:].rearrange("p a b -> p (a b)"), idx[:, bass.ds(n, 4)])
                pl.drain()
            if not (isinstance(n, int) and n < 4):
                pl.wait_ge(ext, n - 3)
                pl.tensor_tensor(spare[:, s:s + 1], ident[0:1, 0:1], ident[0:1, 0:1], ALU.mult)
            if isinstance(i, int) and i == 0:
                pl.wait_ge(mixed, NB - 3 + s)
            pl.indirect_dma_start(xb[:, s, :], None, x_flat,
                                  bass.IndirectOffsetOnAxis(ap=cur_idx[:, s, :], axis=0)).then_inc(gath[s], 16)

        quads(pl, NSLOT, gather)
        attention_gpsimd(pl)

    @block.sync
    def _(sp):
        sp.dma_start(wt_row[:], wt).then_inc(small_in, 16)
        sp.dma_start(wg_row[:], wg).then_inc(small_in, 16)
        sp.dma_start(cond_row[:], cond).then_inc(small_in, 16)

        def load_late(m):
            since(sp, et, m - 1)
            sp.dma_start(xe[:, m % 2, :], x[EARLY + m]).then_inc(xe_in[m % 2], 16)

        load_late(0)
        load_late(1)
        for s in range(4):
            sp.dma_start(xb[:, s, :], x[s]).then_inc(x_in[s], 16)
        for m in range(2, AHEAD + 2):
            load_late(m)
        sp.wait_ge(consts, N_CONST)
        sp.dma_start(ids_dram.rearrange("(a b) o -> a (b o)", b=P), zeros[0:NSLOT, :]).then_inc(ids_zero, 16)

        def store_mix(i, s):
            t = 4 * i + s
            sp.wait_ge(mixed, t + 1)
            sp.dma_start(mix_dram[bass.ts(t, P), :], mixb[:, s % 2, :]).then_inc(mix_out[s % 2], 16)
            if not (isinstance(i, int) and i == NB // 4 - 1):
                sp.dma_start(xb[:, s, :], x[bass.ds(t + 4, 1)].rearrange("a s h -> (a s) h")).then_inc(x_in[s], 16)

        for t in range(EARLY):
            store_mix(t // 4, t % 4)
            if AHEAD + 2 + t < NB - EARLY:
                load_late(AHEAD + 2 + t)
        with sp.Fori(EARLY // 4, NB // 4 - 1) as i:
            for s in range(4):
                store_mix(i, s)
        for s in range(4):
            store_mix(NB // 4 - 1, s)
            if s == 0:
                for q in range(4):
                    sp.wait_ge(scat[q], 2 * 16 * NB // 4)
                sp.dma_start(id_row[:], ids_dram.rearrange("(a b) o -> a (b o)", b=P)).then_inc(ids_row_in, 16)

        sp.wait_ge(idx_ok, 1)
        sp.wait_ge(dd, NB)
        sp.dma_start(bias[:], fside.rearrange("h i j -> i h j")).then_inc(bias_in, 16)
        with nc.allow_non_contiguous_dma(reason="columns of a few hundred elements"):
            sp.dma_start(gin[:], g_in.rearrange("(k p) -> p k", p=P)).then_inc(a_small, 16)
            for j in range(2):
                sp.dma_start(nvc[j * D:(j + 1) * D, :], cond[1:2, :].rearrange("a d -> d a")).then_inc(a_small, 16)
        sp.dma_start(nkb[:], cond[0:1, :].to_broadcast([P, D])).then_inc(a_small, 16)
        sp.dma_start(nbb[:], null_bias.rearrange("(a h) -> a h", a=1).to_broadcast([P, NH])).then_inc(a_small, 16)
        sp.dma_start(mask_in[:], mask).then_inc(a_small, 16)
        sp.dma_start(wkv_raw[:], wkv.rearrange("(k p) n -> p k n", p=P)).then_inc(a_small, 16)
        for k in range(2):
            sp.dma_start(wq_raw[:, k, :], wq[k * P:(k + 1) * P, :]).then_inc(wq_in[k], 16)

        def store_y(i, s):
            n = 4 * i + s
            sp.wait_ge(eyc, n + 1)
            sp.dma_start(ys_dram[bass.ts(n, P), :], yb[:, s % 2, :]).then_inc(ys_out[s % 2], 16)

        for s in range(4):
            store_y(0, s)
        for k in range(KC):
            with sp.Fori(1 + 4 * k, 5 + 4 * k) as i:
                for s in range(4):
                    store_y(i, s)
            if k < 2:
                sp.wait_ge(wq_hi, k + 1)
                sp.wait_ge(null_s, 2 * (k + 1))
                sp.dma_start(wq_raw[:, k, :], wq[(k + 2) * P:(k + 3) * P, :]).then_inc(wq_in[k], 16)
        for s in range(4):
            store_y(NSLOT // 4 - 1, s)
        for s in range(2):
            sp.wait_ge(mix_out[s], 16 * (NB // 2))
            sp.wait_ge(ys_out[s], 16 * (NSLOT // 2))
        attention_sync(sp)

    @block.scalar
    def _(act):
        for j, w in enumerate((sw_gate, sw_up, sw_down)):
            act.dma_start(raw[j][:], w.rearrange("(k p) n -> p k n", p=P)).then_inc(raw_in[j], 16)

        def late_copy(m, bank, buf, read):
            act.wait_ge(et, m + 1)
            since(act, elg, read)
            act.activation(xT0[:, buf], bank[:].rearrange("p (k n) -> p k n", k=KC), ACT.Copy).then_inc(ec, 1)

        for m in range(AHEAD):
            late_copy(m, (T_, D_)[m % 2], m % 2, m - 1)
            if m % 2 and m // 2 < 3:
                act.wait_ge(raw_in[m // 2], 16)
                act.activation(sh_w[m // 2][0][:], raw[m // 2][:], ACT.Copy).then_inc(sh_hi, 1)

        def xhigh(n, par):
            since(act, xt, n + 1)
            since(act, ud, n - 1)
            act.activation(xTh[:, par], T_[:].rearrange("p (k n) -> p k n", k=KC), ACT.Copy).then_inc(xhi, 1)

        def raw_copy(n):
            since(act, xt, n + 1)
            since(act, lg, n)
            act.activation(xT0[:, 0], T_[:].rearrange("p (k n) -> p k n", k=KC), ACT.Copy).then_inc(raw_ok, 1)

        def step1(i, s, early):
            n, par = 4 * i + s, s % 2
            last = isinstance(i, int) and n == NB - 1
            if early:
                raw_copy(n + 1)
            if not last:
                xhigh(n + 1, 1 - par)
            since(act, gd, n + 1)
            since(act, ht, n - 1)
            act.activation(act_h[:, par, :], GB[par][:], ACT.Copy, scale=LEAK).then_inc(sg, 1)
            if early:
                late_copy(AHEAD + n, T_, 1, AHEAD + n)
                if isinstance(i, int):
                    load_expert(n)
            hhigh(n - 1)

        def hhigh(n):
            if isinstance(n, int) and n < 0:
                return
            since(act, ht, n + 1)
            since(act, dd, n)
            act.activation(hTh[:], H_[:].rearrange("p (k n) -> p k n", k=KC), ACT.Copy).then_inc(hhi, 1)

        def load_expert(e):
            for j, w in enumerate((w_gate, w_up)):
                act.dma_start(wgu[:, e, :, j * M:(j + 1) * M], w[e].rearrange("(k p) m -> p k m", p=P)).then_inc(experts_in, 16)
            act.dma_start(wdn[:, e], w_down[e].rearrange("(k p) n -> p k n", p=P)).then_inc(experts_in, 16)

        def after1(t):
            if t < EARLY + 4:
                load_expert(4 + t - EARLY)
            if t == EARLY + 2:
                act.wait_ge(soft_ok, 1)
                act.activation(r["a"][:], r["b"][:], ACT.Exp).then_inc(exp_ok, 1)
                act.activation(c["t"][:], c["p"][:], ACT.Exp).then_inc(exp_ok, 1)

        act.wait_ge(elg, AHEAD)
        raw_copy(0)
        xhigh(0, 0)
        act.wait_ge(sh_lo, 3)
        shared_steps(act, step1, after1)
        hhigh(NB - 1)

        def excopy(n, par):
            since(act, ext, n + 1)
            since(act, egu, n - 1)
            act.activation(xT0[:, par], T_[:].rearrange("p (k n) -> p k n", k=KC), ACT.Copy).then_inc(exc, 1)

        def step2(i, s):
            n, par = 4 * i + s, s % 2
            if not (isinstance(i, int) and n == NSLOT - 1):
                excopy(n + 1, 1 - par)
            since(act, egu, n + 1)
            since(act, eht, n - 1)
            act.activation(eact[:, par, :], GB[par][:, 0:M], ACT.Copy, scale=LEAK).then_inc(esg, 1)
            ycopy(n - 1, 1 - par)

        def ycopy(n, par):
            if isinstance(n, int) and n < 0:
                return
            since(act, edn, n + 1)
            if isinstance(n, int) and n < 2:
                act.wait_ge(mix_out[par], 16 * (NB // 2))
            else:
                act.wait_ge(ys_out[par], 8 * (n - par))
            act.activation(yb[:, par, :], UB[par][:], ACT.Copy).then_inc(eyc, 1)

        excopy(0, 0)
        for s in range(4):
            step2(0, s)
        for k in range(KC):
            with act.Fori(1 + 4 * k, 5 + 4 * k) as i:
                for s in range(4):
                    step2(i, s)
            wq_high(act, k)
        for s in range(4):
            step2(NSLOT // 4 - 1, s)
        ycopy(NSLOT - 1, (NSLOT - 1) % 2)
        attention_scalar(act)

    @block.vector
    def _(dve):
        dve.wait_ge(prep_t, 1)
        dve.tensor_copy(wtT[:], ps[0][:, 0:KC * E].rearrange("p (k e) -> p k e", k=KC)).then_inc(prep_c, 1)
        dve.tensor_copy(wgT[:], ps[1][0:G, 0:E]).then_inc(prep_c, 1)
        dve.tensor_copy(condT[:], ps[1][0:G, E:E + NB]).then_inc(prep_c, 1)

        count = [0]

        def link(ins):
            ins.then_inc(route_v, 1)
            count[0] += 1
            dve.wait_ge(route_v, count[0])

        def over_e(v):
            return v.unsqueeze(2).to_broadcast([P, NB, E])

        def over_t(v):
            return v.unsqueeze(1).to_broadcast([P, NB, E])

        logit, oh1, oh2, ta, tb = (r[k][:] for k in ("logit", "oh1", "oh2", "a", "b"))
        dve.wait_ge(consts, N_CONST)
        dve.wait_ge(prep_t, 2)
        link(dve.tensor_copy(glog[:], ps[1][0:NB, 0:E]))
        dve.tensor_tensor(gdiag[:], ident[0:NB, 0:NB].unsqueeze(2).to_broadcast([NB, NB, E]),
                          glog[:].unsqueeze(1).to_broadcast([NB, NB, E]), ALU.mult).then_inc(prep_c, 1)
        dve.wait_ge(prep_t, 3)
        link(dve.tensor_copy(ta, ps[1][:, 0:NB * E].rearrange("p (t e) -> p t e", e=E)))
        for j in range(3):
            dve.wait_ge(sh_hi, j + 1)
            dve.tensor_tensor(sh_w[j][1][:], raw[j][:], sh_w[j][0][:].bitcast(F32), ALU.subtract).then_inc(sh_lo, 1)
        def first_of(onehot, values, top):
            link(dve.tensor_reduce(top, values, AX.X, ALU.max))
            link(dve.tensor_tensor(ta, values, over_e(top), ALU.is_equal))
            link(dve.tensor_tensor(ta, ta, over_t(rank8[:]), ALU.mult))
            link(dve.tensor_reduce(c["t"][:], ta, AX.X, ALU.max))
            link(dve.tensor_tensor(onehot, ta, over_e(c["t"][:]), ALU.is_equal))

        def first_pick():
            dve.wait_ge(lg, EARLY)
            dve.wait_ge(elg, NB - EARLY)
            link(dve.tensor_tensor(tb, L_[:, 0:NB * E].rearrange("p (t e) -> p t e", e=E), ta, ALU.add))
            link(dve.tensor_scalar(logit, tb, 0.5, None, ALU.mult))
            first_of(oh1, logit, c["max1"][:])

        def second_pick():
            link(dve.scalar_tensor_tensor(tb, oh1, -3.0e38, logit, ALU.mult, ALU.add))
            first_of(oh2, tb, c["max2"][:])
            dve.tensor_tensor(picks[:], oh1, oh2, ALU.add).then_inc(picks_ok, 1)
            link(dve.tensor_tensor(tb, logit, over_e(c["max1"][:]), ALU.subtract))
            dve.tensor_tensor(c["p"][:], c["max2"][:], c["max1"][:], ALU.subtract).then_inc(soft_ok, 1)

        def xlow(n, par):
            since(dve, xhi, n + 1)
            since(dve, ud, n - 1)
            dve.tensor_tensor(xTl[:, par], T_[:].rearrange("p (k n) -> p k n", k=KC), xTh[:, par].bitcast(F32),
                              ALU.subtract).then_inc(xlo, 1)

        def hlow(n):
            if isinstance(n, int) and n < 0:
                return
            since(dve, hhi, n + 1)
            dve.tensor_tensor(hTl[:], H_[:].rearrange("p (k n) -> p k n", k=KC), hTh[:].bitcast(F32),
                              ALU.subtract).then_inc(hlo, 1)

        def leaky(n, par):
            since(dve, sg, n + 1)
            dve.tensor_tensor(act_h[:, par, :], act_h[:, par, :], GB[par][:], ALU.max).then_inc(lk, 1)

        def hidden(n, par):
            since(dve, ud, n + 1)
            since(dve, lk, n + 1)
            dve.tensor_tensor(act_h[:, par, :], act_h[:, par, :], UB[par][:], ALU.mult).then_inc(hd, 1)

        def mix(n, par, slot):
            if isinstance(n, int) and n < 0:
                return
            since(dve, dd, n + 1)
            if not (isinstance(n, int) and n < 2):
                dve.wait_ge(mix_out[par], 8 * (n - par))
            dve.tensor_tensor(mixb[:, par, :], xb[:, slot, :], D_[:], ALU.add).then_inc(mixed, 1)

        def step1(i, s, early):
            n, par = 4 * i + s, s % 2
            if not (isinstance(i, int) and n == NB - 1):
                xlow(n + 1, 1 - par)
            leaky(n, par)
            hlow(n - 1)
            hidden(n, par)
            mix(n - 1, 1 - par, (s + 3) % 4)

        def weights_of_tokens():
            dve.wait_ge(exp_ok, 2)
            link(dve.tensor_reduce(c["sum"][:], ta, AX.X, ALU.add))
            link(dve.reciprocal(c["sum"][:], c["sum"][:]))
            link(dve.tensor_tensor(c["w2"][:], c["t"][:], c["sum"][:], ALU.mult))
            link(dve.scalar_tensor_tensor(c["p"][:], c["sum"][:], TINY, c["w2"][:], ALU.add, ALU.add))
            link(dve.reciprocal(c["p"][:], c["p"][:]))
            link(dve.tensor_tensor(c["w1"][:], c["sum"][:], c["p"][:], ALU.mult))
            link(dve.tensor_tensor(c["w2"][:], c["w2"][:], c["p"][:], ALU.mult))

        def expert_bases():
            dve.wait_ge(ranks_ok, 1)
            link(dve.tensor_copy(ta, L_[:, NB * E:2 * NB * E].rearrange("p (t e) -> p t e", e=E)))
            link(dve.memset(small["z"][:], 0.0))
            zero_col = small["z"][:, 0:1].to_broadcast([P, NB])
            for e in range(E):
                step = dve.tensor_tensor_scan(tb[:, :, e], ta[:, :, e], zero_col, 0.0, ALU.add, ALU.add)
            link(step)
            link(dve.tensor_copy(small["n"][:], tb[:, NB - 1, :]))
            link(dve.tensor_tensor(many[:], small["n"][:].unsqueeze(2).to_broadcast([P, E, MAXT - 1]),
                                   steps128[:].unsqueeze(1).to_broadcast([P, E, MAXT - 1]), ALU.is_gt))
            link(dve.tensor_reduce(small["tiles"][:], many[:], AX.X, ALU.add))
            link(dve.tensor_scalar(small["tiles"][:], small["tiles"][:], 1.0, None, ALU.add))
            link(dve.tensor_tensor_scan(small["ends"][:], small["tiles"][:], small["z"][:], 0.0, ALU.add, ALU.add))
            link(dve.tensor_tensor(small["base"][:], small["ends"][:], small["tiles"][:], ALU.subtract))
            link(dve.tensor_scalar(small["base"][:], small["base"][:], float(P), None, ALU.mult))

        def slots_of_tokens():
            link(dve.tensor_tensor(tb, tb, ta, ALU.subtract))
            link(dve.tensor_tensor(ta, tb, over_t(small["base"][:]), ALU.add))
            link(dve.tensor_tensor(tb, ta, L_[:, 0:NB * E].rearrange("p (t e) -> p t e", e=E), ALU.add))
            for k, oh in enumerate((oh1, oh2)):
                link(dve.tensor_tensor(ta, tb, oh, ALU.mult))
                link(dve.tensor_reduce(c["t"][:], ta, AX.X, ALU.add))
                step = dve.tensor_copy(pos[:, :, k], c["t"][:])
                if k:
                    step.then_inc(pos_ok, 1)
                else:
                    link(step)
            link(dve.tensor_tensor(per_slot[:], slots[:].unsqueeze(2).to_broadcast([P, NSLOT, E - 1]),
                                   small["ends"][:, 0:E - 1].unsqueeze(1).to_broadcast([P, NSLOT, E - 1]), ALU.is_ge))
            link(dve.tensor_reduce(many_flat, per_slot[:], AX.X, ALU.add))
            dve.tensor_copy(e_of_slot[:, 4:], many_flat).then_inc(route_v, 1)
            count[0] += 1

        many_flat = many[:].rearrange("p a b -> p (a b)")[:, 0:NSLOT]
        xlow(0, 0)

        def after1(t):
            if t == EARLY:
                first_pick()
            if t == EARLY + 1:
                second_pick()
            if t == EARLY + 2:
                weights_of_tokens()
                expert_bases()
            if t == EARLY + 3:
                slots_of_tokens()
            if t == NB - 2:
                dve.wait_ge(ids_T, 1)
                dve.tensor_copy(idx[:], L_[:, 0:NSLOT]).then_inc(idx_ok, 1)

        shared_steps(dve, step1, after1)
        hlow(NB - 1)
        mix(NB - 1, (NB - 1) % 2, 3)
        names["route_total"] = count[0]

        def ehcopy(n, par):
            if isinstance(n, int) and n < 0:
                return
            since(dve, eht, n + 1)
            since(dve, edn, n - 1)
            dve.tensor_copy(ehT[:, par], H_[:, 0:M].rearrange("p (k n) -> p k n", k=MC)).then_inc(ehc, 1)

        def step2(i, s):
            n, par = 4 * i + s, s % 2
            ehcopy(n - 1, 1 - par)
            since(dve, esg, n + 1)
            dve.tensor_tensor(eact[:, par, :], eact[:, par, :], GB[par][:, 0:M], ALU.max).then_inc(elk, 1)
            since(dve, elk, n + 1)
            dve.tensor_tensor(eact[:, par, :], eact[:, par, :], GB[par][:, M:2 * M], ALU.mult).then_inc(ehd, 1)

        for s in range(4):
            step2(0, s)
        for k in range(KC):
            with dve.Fori(1 + 4 * k, 5 + 4 * k) as i:
                for s in range(4):
                    step2(i, s)
            wq_low(dve, k)
        for s in range(4):
            step2(NSLOT // 4 - 1, s)
        ehcopy(NSLOT - 1, (NSLOT - 1) % 2)
        attention_vector(dve)

    @block.tensor
    def _(pe):
        pe.wait_ge(consts, N_CONST)
        pe.wait_ge(small_in, 16 * N_SMALL)
        for k in range(KC):
            pe.transpose(ps[0][:, k * E:(k + 1) * E], wt_row[:, k * P:(k + 1) * P], ident[0:E, 0:E])
        pe.transpose(ps[1][0:G, 0:E], wg_row[:], ident[0:E, 0:E])
        pe.transpose(ps[1][0:G, E:E + NB], cond_row[:], ident[0:NB, 0:NB]).then_inc(prep_t, 1)
        pe.wait_ge(prep_c, 3)

        def late_turn(m, par, bank):
            pe.wait_ge(xe_in[par], 8 * (m - par) + 16)
            for k in range(KC):
                mm = pe.transpose(bank[:, k * P:(k + 1) * P], xe[:, par, k * P:(k + 1) * P], ident[:])
            mm.then_inc(et, 1)

        def logits(t, buf, done):
            o = L_[:, bass.ds(t * E, E)]
            for k in range(KC):
                mm = pe.matmul(o, xT0[:, buf, k, :], wtT[:, k, :], start=(k == 0), stop=(k == KC - 1))
            mm.then_inc(done, 1)

        for m in range(AHEAD + 1):
            if m < AHEAD:
                since(pe, ec, m - 1)
                late_turn(m, m % 2, (T_, D_)[m % 2])
            if m == 1:
                pe.matmul(H_[0:NB, 0:E], condT[:], wgT[:], start=True, stop=True).then_inc(prep_t, 1)
            if m == 3:
                pe.wait_ge(prep_c, 4)
                pe.matmul(H_[:, 0:NB * E], ones_f[:], gdiag[:].rearrange("p t e -> p (t e)"),
                          start=True, stop=True).then_inc(prep_t, 1)
            if m:
                pe.wait_ge(ec, m)
                logits(EARLY + m - 1, (m - 1) % 2, elg)
        pe.wait_ge(route_v, 2)

        def turn(i, s, early):
            n = 4 * i + s
            pe.wait_ge(x_in[s], 16 * (i + 1))
            since(pe, xlo, n)
            if early:
                since(pe, ec, AHEAD if isinstance(n, int) and n == 0 else AHEAD - 1 + n)
            elif isinstance(n, int) and n == EARLY + 1:
                pe.wait_ge(ec, NB - EARLY)
                pe.wait_ge(raw_ok, EARLY + 1)
            for k in range(KC):
                mm = pe.transpose(T_[:, k * P:(k + 1) * P], xb[:, s, k * P:(k + 1) * P], ident[:])
            mm.then_inc(xt, 1)

        def turn_h(n, par):
            if isinstance(n, int) and n < 0:
                return
            since(pe, hd, n + 1)
            since(pe, hlo, n)
            for k in range(KC):
                mm = pe.transpose(H_[:, k * P:(k + 1) * P], act_h[:, par, k * P:(k + 1) * P], ident[:])
            mm.then_inc(ht, 1)

        def project(bank, par, w):
            for k in range(KC):
                mm = split3(pe, bank[:], (xTh[:, par, k], xTl[:, par, k]), (w[0][:, k], w[1][:, k]),
                            k == 0, k == KC - 1)
            return mm

        def down(n):
            if isinstance(n, int) and n < 0:
                return
            since(pe, hlo, n + 1)
            since(pe, mixed, n)
            for k in range(KC):
                mm = split3(pe, D_[:], (hTh[:, k], hTl[:, k]), (sh_w[2][0][:, k], sh_w[2][1][:, k]),
                            k == 0, k == KC - 1)
            mm.then_inc(dd, 1)

        def step1(i, s, early):
            n, par = 4 * i + s, s % 2
            if not (isinstance(i, int) and n == NB - 1):
                turn(i + (s == 3), (s + 1) % 4, early)
            if early:
                since(pe, raw_ok, n + 1)
                logits(n, 0, lg)
            since(pe, xlo, n + 1)
            since(pe, lk, n - 1)
            project(GB[par], par, sh_w[0]).then_inc(gd, 1)
            turn_h(n - 1, 1 - par)
            if early:
                pe.wait_ge(xlo, n + 2)
                pe.wait_ge(raw_ok, n + 2)
                late_turn(AHEAD + n, par, T_)
            since(pe, hd, n - 1)
            project(UB[par], par, sh_w[1]).then_inc(ud, 1)
            if early:
                pe.wait_ge(ec, AHEAD + n + 1)
                logits(EARLY + AHEAD + n, 1, elg)
            down(n - 1)

        def after1(t):
            if t == EARLY + 2:
                pe.wait_ge(picks_ok, 1)
                pe.matmul(L_[:, 0:NB * E], below[:], picks[:].rearrange("p t e -> p (t e)"), start=True, stop=True)
                pe.matmul(L_[:, NB * E:2 * NB * E], ones_b[:], picks[:].rearrange("p t e -> p (t e)"),
                          start=True, stop=True).then_inc(ranks_ok, 1)
            if t == NB - 2:
                pe.wait_ge(ids_row_in, 16)
                pe.transpose(L_[:, 0:NSLOT], id_row[:], ident[0:NSLOT, 0:NSLOT]).then_inc(ids_T, 1)

        turn(0, 0, True)
        pe.wait_ge(sh_lo, 3)
        shared_steps(pe, step1, after1)
        def eturn(i, s):
            n = 4 * i + s
            pe.wait_ge(gath[s], 16 * (i + 1))
            since(pe, exc, n)
            for k in range(KC):
                mm = pe.transpose(T_[:, k * P:(k + 1) * P], xb[:, s, k * P:(k + 1) * P], ident[:])
            mm.then_inc(ext, 1)

        def eturn_h(n, par):
            if isinstance(n, int) and n < 0:
                return
            since(pe, ehd, n + 1)
            since(pe, ehc, n)
            for k in range(MC):
                mm = pe.transpose(H_[:, k * P:(k + 1) * P], eact[:, par, k * P:(k + 1) * P], ident[:])
            mm.then_inc(eht, 1)

        def edown(n, par, e):
            if isinstance(n, int) and n < 0:
                return
            since(pe, ehc, n + 1)
            since(pe, eyc, n - 1)
            for k in range(MC):
                mm = pe.matmul(UB[par][:], ehT[:, par, k], wdn[:, bass.ds(e, 1), k, :].rearrange("p a n -> p (a n)"),
                               start=(k == 0), stop=(k == MC - 1))
            mm.then_inc(edn, 1)

        def expert(n):
            return pe.value_load(e_of_slot[0:1, bass.ds(4 + n, 1)], min_val=0, max_val=E - 1)

        def step2(i, s, e_prev):
            n, par = 4 * i + s, s % 2
            if not (isinstance(i, int) and n == NSLOT - 1):
                eturn(i + (s == 3), (s + 1) % 4)
            e = expert(n)
            if s == 0 and not (isinstance(i, int) and i == 0):
                e_prev = expert(n - 1)
            since(pe, exc, n + 1)
            since(pe, ehd, n - 1)
            for k in range(KC):
                if k == KC // 2:
                    eturn_h(n - 1, 1 - par)
                mm = pe.matmul(GB[par][:], xT0[:, par, k], wgu[:, bass.ds(e, 1), k, :].rearrange("p a n -> p (a n)"),
                               start=(k == 0), stop=(k == KC - 1))
            mm.then_inc(egu, 1)
            edown(n - 1, 1 - par, e_prev)
            return e

        pe.wait_ge(experts_in, 16 * 3 * E)
        pe.wait_ge(route_v, names["route_total"])
        pe.wait_ge(xlo, NB)
        eturn(0, 0)
        turn_h(NB - 1, (NB - 1) % 2)
        down(NB - 1)
        pe.wait_ge(hlo, NB)
        pe.wait_ge(hd, NB)
        held = [None]

        def body(i, s):
            held[0] = step2(i, s, held[0])

        quads(pe, NSLOT, body)
        edown_h = (NSLOT - 1) % 2
        eturn_h(NSLOT - 1, edown_h)
        edown(NSLOT - 1, edown_h, held[0])
        attention_tensor(pe)
    ctx.close()


def kernel(x, cond_64, fside_16xSxS_0, mask_BxS_bk0, L0_cond_wt, L0_cond_wg, L0_cond_w_gate, L0_cond_w_up,
           L0_cond_w_down, L0_cond_sw_gate, L0_cond_sw_up, L0_cond_sw_down, L1_cond_g_in,
           L1_cond_null_attn_bias, L1_cond_Wq, L1_cond_Wkv, L1_cond_Wo, L1_cond_g_out):
    import numpy as np

    import concourse.bacc as bacc
    from concourse.bass_utils import run_bass_kernel_spmd

    arrays = {"x": x, "cond": cond_64, "attn_bias": fside_16xSxS_0, "mask": np.ascontiguousarray(mask_BxS_bk0).view(np.int32),
              "wt": L0_cond_wt, "wg": L0_cond_wg, "w_gate": L0_cond_w_gate, "w_up": L0_cond_w_up,
              "w_down": L0_cond_w_down, "sw_gate": L0_cond_sw_gate, "sw_up": L0_cond_sw_up,
              "sw_down": L0_cond_sw_down, "g_in": L1_cond_g_in, "null_attn_bias": L1_cond_null_attn_bias,
              "wq": L1_cond_Wq, "wkv": L1_cond_Wkv, "wo": L1_cond_Wo, "g_out": L1_cond_g_out}
    arrays = {name: np.asarray(a) for name, a in arrays.items()}
    nc = bacc.Bacc("TRN2", target_bir_lowering=False, num_devices=1)
    ins = [nc.dram_tensor(f"in_{name}_dram", a.shape, mybir.dt.from_np(a.dtype), kind="ExternalInput").ap()
           for name, a in arrays.items()]
    out = nc.dram_tensor("out_dram", arrays["x"].shape, F32, kind="ExternalOutput").ap()
    moe_attention(nc, *ins, out)
    nc.compile()
    res = run_bass_kernel_spmd(nc, [{f"in_{name}_dram": a for name, a in arrays.items()}], core_ids=[0])
    return res.results[0]["out_dram"]
```
